# Optimizing a Trainium2 kernel written in Bass

```python
import numpy as np
import jax
import jax.numpy as jnp

def _softmax(x, axis=-1):
    return jax.nn.softmax(x, axis=axis)

def _gelu(x):
    return jax.nn.gelu(x, approximate=True)

def _silu(x):
    return jax.nn.silu(x)

def _sigmoid(x):
    return jax.nn.sigmoid(x)

def _layernorm(x, axis=-1, eps=1e-05):
    m = jnp.mean(x, axis=axis, keepdims=True)
    v = jnp.var(x, axis=axis, keepdims=True)
    return (x - m) / jnp.sqrt(v + eps)

def _scatter_add(tgt, idx, src, axis=0):
    return tgt.at[idx].add(src)

def _segment_sum(src, seg, n):
    return jax.ops.segment_sum(src, seg, n)
kernel_name = 'mk_adaln_d2_jaxref_r4_c640fb'

def setup_inputs(seed: int=0):
    np.random.seed(seed)
    _w = jnp.asarray

    def _L0_attn_setup():
        import jax, jax.numpy as jnp
        import numpy as np
        B, L, H, I, K, G = (2, 1024, 256, 512, 4, 8)
        EPS = 1e-05

        def _layernorm(x, g, b):
            m = x.mean(-1, keepdims=True)
            v = jnp.var(x, axis=-1, keepdims=True)
            return (x - m) * jax.lax.rsqrt(v + EPS) * g + b
        key = jax.random.key(seed)
        ks = jax.random.split(key, 8)
        s = 0.02
        return {'hidden_states': jax.random.normal(ks[0], (B, L, H), jnp.float32), 'in_proj_w': jax.random.normal(ks[1], (2 * I, H), jnp.float32) * s, 'conv_w': jax.random.normal(ks[2], (I, I // G, K), jnp.float32) * s, 'conv_b': jax.random.normal(ks[3], (I,), jnp.float32) * s, 'ln_g': jnp.ones((I,), jnp.float32), 'ln_b': jnp.zeros((I,), jnp.float32), 'fc_w': jax.random.normal(ks[4], (H, I), jnp.float32) * s, 'fc_b': jnp.zeros((H,), jnp.float32), 'cproj_w': jax.random.normal(ks[5], (I, H), jnp.float32) * s, 'cproj_b': jnp.zeros((I,), jnp.float32), 'out_w': jax.random.normal(ks[6], (H, I), jnp.float32) * s}
    _L0_attn_in = _L0_attn_setup()

    def _L0_ffn_setup():
        import jax, jax.numpy as jnp
        import numpy as np
        from jax import lax
        T, B, I, M, O = (64, 64, 256, 256, 256)

        def _xavier(key, shape):
            fan_out, fan_in = shape
            limit = float(np.sqrt(6.0 / (fan_in + fan_out)))
            return jax.random.uniform(key, shape, jnp.float32, -limit, limit)
        key = jax.random.key(seed)
        ks = jax.random.split(key, 9)
        x = jax.random.normal(ks[0], (T, B, I), jnp.float32)
        return {'x': x, 'wf': _xavier(ks[1], (M, I)), 'uf': _xavier(ks[2], (M, M)), 'bf': jnp.zeros((M,), jnp.float32), 'wi': _xavier(ks[3], (M, I)), 'ui': _xavier(ks[4], (M, M)), 'bi': jnp.zeros((M,), jnp.float32), 'wc': _xavier(ks[5], (M, I)), 'uc': _xavier(ks[6], (M, M)), 'bc': jnp.zeros((M,), jnp.float32), 'wo': _xavier(ks[7], (O, I)), 'uo': _xavier(ks[8], (O, M)), 'bo': jnp.zeros((O,), jnp.float32), 'in_c': jnp.zeros((M,), jnp.float32)}
    _L0_ffn_in = _L0_ffn_setup()
    _L0_c = _w((lambda *s: np.random.randn(*s).astype(np.float32) * 0.05)(16, 256))
    _L0_wmod = _w((lambda *s: np.random.randn(*s).astype(np.float32) * 0.05)(256, 6 * 256) * 256 ** (-0.5))

    def _L1_attn_setup():
        import jax, jax.numpy as jnp
        import numpy as np
        import math
        B, T, C, H = (2, 512, 256, 16)
        HD = C // H
        SCALE = 1.0 / math.sqrt(HD)

        def _e8_head_dirs(n_heads: int) -> np.ndarray:
            roots = []
            for i in range(8):
                for j in range(i + 1, 8):
                    for si in (-1.0, 1.0):
                        for sj in (-1.0, 1.0):
                            r = np.zeros(8, dtype=np.float32)
                            r[i] = si
                            r[j] = sj
                            roots.append(r)
            roots = np.stack(roots)
            roots = roots / np.linalg.norm(roots, axis=1, keepdims=True)
            return roots[:n_heads]
        key = jax.random.key(seed)
        k1, k2, k3, k4 = jax.random.split(key, 4)
        x = jax.random.normal(k1, (B, T, C), dtype=jnp.float32)
        w_qkv = jax.random.normal(k2, (C, 3 * C), dtype=jnp.float32) * (1.0 / math.sqrt(C))
        w_out = jax.random.normal(k3, (C, C), dtype=jnp.float32) * (1.0 / math.sqrt(C))
        head_scales = jax.random.normal(k4, (H,), dtype=jnp.float32) * 0.1
        head_dirs = jnp.asarray(_e8_head_dirs(H))
        return {'x': x, 'w_qkv': w_qkv, 'w_out': w_out, 'head_scales': head_scales, 'head_dirs': head_dirs}
    _L1_attn_in = _L1_attn_setup()

    def _L1_ffn_setup():
        import jax, jax.numpy as jnp
        import numpy as np
        B, S, H = (4, 512, 256)
        E = 8
        GS = 2
        NG = E // GS
        F = int(H * 4 * (2.0 / 3.0))
        key = jax.random.key(seed)
        ks = jax.random.split(key, 7)
        sc_h = 1.0 / np.sqrt(H)
        sc_f = 1.0 / np.sqrt(F)
        return {'x': jax.random.normal(ks[0], (B, S, H), dtype=jnp.float32), 'Wr': jax.random.normal(ks[1], (H, E), dtype=jnp.float32) * sc_h, 'br': jnp.zeros((E,), dtype=jnp.float32), 'W_up': jax.random.normal(ks[2], (NG, H, F), dtype=jnp.float32) * sc_h, 'b_up': jax.random.normal(ks[3], (NG, F), dtype=jnp.float32) * 0.01, 'W_down': jax.random.normal(ks[4], (E, F, H), dtype=jnp.float32) * sc_f, 'b_down': jax.random.normal(ks[5], (E, H), dtype=jnp.float32) * 0.01}
    _L1_ffn_in = _L1_ffn_setup()
    _L1_c = _w((lambda *s: np.random.randn(*s).astype(np.float32) * 0.05)(16, 256))
    _L1_wmod = _w((lambda *s: np.random.randn(*s).astype(np.float32) * 0.05)(256, 6 * 256) * 256 ** (-0.5))
    _d = {'L0_attn_hidden_states': _L0_attn_in['hidden_states'], 'L0_attn_in_proj_w': _L0_attn_in['in_proj_w'], 'L0_attn_conv_w': _L0_attn_in['conv_w'], 'L0_attn_conv_b': _L0_attn_in['conv_b'], 'L0_attn_ln_g': _L0_attn_in['ln_g'], 'L0_attn_ln_b': _L0_attn_in['ln_b'], 'L0_attn_fc_w': _L0_attn_in['fc_w'], 'L0_attn_fc_b': _L0_attn_in['fc_b'], 'L0_attn_cproj_w': _L0_attn_in['cproj_w'], 'L0_attn_cproj_b': _L0_attn_in['cproj_b'], 'L0_attn_out_w': _L0_attn_in['out_w'], 'L0_ffn_wf': _L0_ffn_in['wf'], 'L0_ffn_uf': _L0_ffn_in['uf'], 'L0_ffn_bf': _L0_ffn_in['bf'], 'L0_ffn_wi': _L0_ffn_in['wi'], 'L0_ffn_ui': _L0_ffn_in['ui'], 'L0_ffn_bi': _L0_ffn_in['bi'], 'L0_ffn_wc': _L0_ffn_in['wc'], 'L0_ffn_uc': _L0_ffn_in['uc'], 'L0_ffn_bc': _L0_ffn_in['bc'], 'L0_ffn_wo': _L0_ffn_in['wo'], 'L0_ffn_uo': _L0_ffn_in['uo'], 'L0_ffn_bo': _L0_ffn_in['bo'], 'L0_ffn_in_c': _L0_ffn_in['in_c'], 'L0_c': _L0_c, 'L0_wmod': _L0_wmod, 'L1_attn_w_qkv': _L1_attn_in['w_qkv'], 'L1_attn_w_out': _L1_attn_in['w_out'], 'L1_attn_head_scales': _L1_attn_in['head_scales'], 'L1_attn_head_dirs': _L1_attn_in['head_dirs'], 'L1_ffn_Wr': _L1_ffn_in['Wr'], 'L1_ffn_br': _L1_ffn_in['br'], 'L1_ffn_W_up': _L1_ffn_in['W_up'], 'L1_ffn_b_up': _L1_ffn_in['b_up'], 'L1_ffn_W_down': _L1_ffn_in['W_down'], 'L1_ffn_b_down': _L1_ffn_in['b_down'], 'L1_c': _L1_c, 'L1_wmod': _L1_wmod}
    _x0 = _d['L0_attn_hidden_states']
    _d['L0_attn_hidden_states'] = jax.random.normal(jax.random.fold_in(jax.random.key(seed), 1), (16, 512, 256), dtype=_x0.dtype)
    del _x0
    return _d

def reference(L0_attn_hidden_states, L0_attn_in_proj_w, L0_attn_conv_w, L0_attn_conv_b, L0_attn_ln_g, L0_attn_ln_b, L0_attn_fc_w, L0_attn_fc_b, L0_attn_cproj_w, L0_attn_cproj_b, L0_attn_out_w, L0_ffn_wf, L0_ffn_uf, L0_ffn_bf, L0_ffn_wi, L0_ffn_ui, L0_ffn_bi, L0_ffn_wc, L0_ffn_uc, L0_ffn_bc, L0_ffn_wo, L0_ffn_uo, L0_ffn_bo, L0_ffn_in_c, L0_c, L0_wmod, L1_attn_w_qkv, L1_attn_w_out, L1_attn_head_scales, L1_attn_head_dirs, L1_ffn_Wr, L1_ffn_br, L1_ffn_W_up, L1_ffn_b_up, L1_ffn_W_down, L1_ffn_b_down, L1_c, L1_wmod):

    def _L0_attn_ref(hidden_states, in_proj_w, conv_w, conv_b, ln_g, ln_b, fc_w, fc_b, cproj_w, cproj_b, out_w):
        import jax, jax.numpy as jnp
        import numpy as np
        B, L, H, I, K, G = (2, 1024, 256, 512, 4, 8)
        EPS = 1e-05

        def _layernorm(x, g, b):
            m = x.mean(-1, keepdims=True)
            v = jnp.var(x, axis=-1, keepdims=True)
            return (x - m) * jax.lax.rsqrt(v + EPS) * g + b
        p = hidden_states @ in_proj_w.T
        h, gate = (p[..., :I], p[..., I:])
        gate = jax.nn.silu(gate)
        hc = jnp.transpose(h, (0, 2, 1))
        conv = jax.lax.conv_general_dilated(hc, conv_w, window_strides=(1,), padding=[(K - 1, 0)], feature_group_count=G, dimension_numbers=('NCH', 'OIH', 'NCH'))
        conv = conv + conv_b[None, :, None]
        h = jnp.transpose(conv, (0, 2, 1)) * gate
        residual = h
        hn = _layernorm(h, ln_g, ln_b)
        m = jax.nn.silu(hn @ fc_w.T + fc_b) @ cproj_w.T + cproj_b
        h = m + residual
        return h @ out_w.T

    def _L0_ffn_ref(x, wf, uf, bf, wi, ui, bi, wc, uc, bc, wo, uo, bo, in_c):
        import jax, jax.numpy as jnp
        import numpy as np
        from jax import lax
        T, B, I, M, O = (64, 64, 256, 256, 256)

        def _xavier(key, shape):
            fan_out, fan_in = shape
            limit = float(np.sqrt(6.0 / (fan_in + fan_out)))
            return jax.random.uniform(key, shape, jnp.float32, -limit, limit)
        batch = x.shape[1]
        c0 = jnp.broadcast_to(in_c, (batch, in_c.shape[0]))

        def step(c, xt):
            ft = jax.nn.sigmoid(xt @ wf.T + c @ uf.T + bf)
            it = jax.nn.sigmoid(xt @ wi.T + c @ ui.T + bi)
            gt = jnp.tanh(xt @ wc.T + c @ uc.T + bc)
            c = ft * c + it * gt
            return (c, None)
        c_final, _ = lax.scan(step, c0, x)
        h = jnp.tanh(jnp.einsum('tbi,oi->tbo', x, wo) + c_final @ uo.T + bo)
        return h

    def _L1_attn_ref(x, w_qkv, w_out, head_scales, head_dirs):
        import jax, jax.numpy as jnp
        import numpy as np
        import math
        B, T, C, H = (2, 512, 256, 16)
        HD = C // H
        SCALE = 1.0 / math.sqrt(HD)

        def _e8_head_dirs(n_heads: int) -> np.ndarray:
            roots = []
            for i in range(8):
                for j in range(i + 1, 8):
                    for si in (-1.0, 1.0):
                        for sj in (-1.0, 1.0):
                            r = np.zeros(8, dtype=np.float32)
                            r[i] = si
                            r[j] = sj
                            roots.append(r)
            roots = np.stack(roots)
            roots = roots / np.linalg.norm(roots, axis=1, keepdims=True)
            return roots[:n_heads]
        Bx, Tx, Cx = x.shape
        qkv = (x @ w_qkv).reshape(Bx, Tx, 3, H, HD)
        qkv = jnp.transpose(qkv, (2, 0, 3, 1, 4))
        q, k, v = (qkv[0], qkv[1], qkv[2])
        scores = jnp.einsum('bhqd,bhkd->bhqk', q, k) * SCALE
        causal = jnp.tril(jnp.ones((Tx, Tx), dtype=bool))
        scores = jnp.where(causal[None, None], scores, -jnp.inf)
        q_proj = jnp.einsum('bhtd,hd->bht', q[..., :8], head_dirs)
        k_proj = jnp.einsum('bhtd,hd->bht', k[..., :8], head_dirs)
        geo_bias = q_proj[..., :, None] * k_proj[..., None, :]
        scores = scores + head_scales[None, :, None, None] * geo_bias
        attn = jax.nn.softmax(scores, axis=-1)
        out = jnp.einsum('bhqk,bhkd->bhqd', attn, v)
        out = jnp.transpose(out, (0, 2, 1, 3)).reshape(Bx, Tx, Cx)
        return out @ w_out

    def _L1_ffn_ref(x, Wr, br, W_up, b_up, W_down, b_down):
        import jax, jax.numpy as jnp
        import numpy as np
        B, S, H = (4, 512, 256)
        E = 8
        GS = 2
        NG = E // GS
        F = int(H * 4 * (2.0 / 3.0))
        b, s, h = x.shape
        n_tok = b * s
        k = n_tok // E
        xf = x.reshape(n_tok, h)
        logits = xf @ Wr + br
        Sm = jax.nn.softmax(logits, axis=-1)
        G_t, idx_t = jax.lax.top_k(Sm.T, k)
        G = G_t.T
        idx = idx_t.T
        tokens = xf[idx]
        group = jnp.arange(E) // GS
        Wu = W_up[group]
        bu = b_up[group]
        mid = jax.nn.silu(jnp.einsum('keh,ehf->kef', tokens, Wu) + bu)
        out = jnp.einsum('kef,efh->keh', mid, W_down) + b_down
        y = jnp.zeros_like(xf).at[idx].add(G[..., None] * out)
        return y.reshape(b, s, h)
    x = L0_attn_hidden_states
    mod = (_silu(L0_c) @ L0_wmod).reshape(L0_c.shape[0], 6, 1, -1)
    sa, ca, ga, sb, cb, gb = (mod[:, 0], mod[:, 1], mod[:, 2], mod[:, 3], mod[:, 4], mod[:, 5])
    ga = (2 * (ga >= 0) - 1) * jnp.maximum(jnp.abs(ga), 0.25)
    gb = (2 * (gb >= 0) - 1) * jnp.maximum(jnp.abs(gb), 0.25)
    h = _layernorm(x, axis=-1) * (1 + ca) + sa
    x = x + ga * _L0_attn_ref(h, L0_attn_in_proj_w, L0_attn_conv_w, L0_attn_conv_b, L0_attn_ln_g, L0_attn_ln_b, L0_attn_fc_w, L0_attn_fc_b, L0_attn_cproj_w, L0_attn_cproj_b, L0_attn_out_w)
    h = _layernorm(x, axis=-1) * (1 + cb) + sb
    x = x + gb * _L0_ffn_ref(h, L0_ffn_wf, L0_ffn_uf, L0_ffn_bf, L0_ffn_wi, L0_ffn_ui, L0_ffn_bi, L0_ffn_wc, L0_ffn_uc, L0_ffn_bc, L0_ffn_wo, L0_ffn_uo, L0_ffn_bo, L0_ffn_in_c)
    mod = (_silu(L1_c) @ L1_wmod).reshape(L1_c.shape[0], 6, 1, -1)
    sa, ca, ga, sb, cb, gb = (mod[:, 0], mod[:, 1], mod[:, 2], mod[:, 3], mod[:, 4], mod[:, 5])
    ga = (2 * (ga >= 0) - 1) * jnp.maximum(jnp.abs(ga), 0.25)
    gb = (2 * (gb >= 0) - 1) * jnp.maximum(jnp.abs(gb), 0.25)
    h = _layernorm(x, axis=-1) * (1 + ca) + sa
    x = x + ga * _L1_attn_ref(h, L1_attn_w_qkv, L1_attn_w_out, L1_attn_head_scales, L1_attn_head_dirs)
    h = _layernorm(x, axis=-1) * (1 + cb) + sb
    x = x + gb * _L1_ffn_ref(h, L1_ffn_Wr, L1_ffn_br, L1_ffn_W_up, L1_ffn_b_up, L1_ffn_W_down, L1_ffn_b_down)
    return x

_drawn_inputs = setup_inputs


def setup_inputs(seed=0):
    import zlib

    import numpy as np

    out = dict(_drawn_inputs(seed))
    spreads = {'L0_attn_ln_g': (1.0, 0.6),
     'L0_attn_ln_b': (0.0, 0.8),
     'L0_attn_fc_b': (0.0, 0.8),
     'L0_attn_cproj_b': (0.0, 0.6),
     'L0_ffn_bf': (0.0, 0.8),
     'L0_ffn_bi': (0.0, 0.8),
     'L0_ffn_bc': (0.0, 0.564),
     'L0_ffn_bo': (0.0, 1.845),
     'L0_ffn_in_c': (0.0, 0.8),
     'L1_ffn_br': (0.0, 2.0)}
    factors = {'L0_attn_in_proj_w': 5.836,
     'L0_attn_conv_w': 5.895,
     'L0_attn_conv_b': 8.0,
     'L0_attn_fc_w': 5.948,
     'L0_attn_cproj_w': 5.727,
     'L0_attn_out_w': 3.456,
     'L0_ffn_uf': 4.352,
     'L0_ffn_ui': 3.627,
     'L1_attn_head_scales': 8.0,
     'L1_attn_head_dirs': 8.0,
     'L1_ffn_b_up': 64.0,
     'L1_ffn_b_down': 64.0,
     'L1_ffn_Wr': 3.02,
     'L1_ffn_W_up': 3.042,
     'L1_ffn_W_down': 2.845}
    for name, (base, spread) in spreads.items():
        noise = np.random.default_rng([zlib.crc32(name.encode()), seed]).standard_normal(out[name].shape)
        drawn = base * np.exp(spread * noise) if base else spread * noise
        out[name] = jnp.asarray(drawn.astype(out[name].dtype))
    for name, factor in factors.items():
        out[name] = (out[name] * factor).astype(out[name].dtype)
    return out
```

```python
from contextlib import ExitStack

import numpy as np

import concourse.bass as bass
from concourse import mybir

F32 = mybir.dt.float32
F32R = mybir.dt.float32r
BF16 = mybir.dt.bfloat16
I32 = mybir.dt.int32
U32 = mybir.dt.uint32
ALU = mybir.AluOpType
ACT = mybir.ActivationFunctionType
AX = mybir.AxisListType

P = 128
NB = 16
T = 512
TT = T // P
D = 256
DK = D // P
NT = NB * TT
INNER = 512
IK = INNER // P
TAPS = 4
EPS = 1e-5
BANK = 512

SHIFT_A, SCALE_A, GATE_A, SHIFT_B, SCALE_B, GATE_B = 0, 2, 4, 6, 8, 10


class Signal:

    def __init__(self, ctx, nc, name, per=1, before=0):
        self.sem = ctx.enter_context(nc.semaphore(name))
        self.per, self.before = per, before

    def __call__(self, i, k):
        return self.sem, i * self.per + (self.before + k)


def product3(pe, out, w, x, start, stop):
    pe.matmul(out, w[0], x[0], start=start, stop=False)
    pe.matmul(out, w[0], x[1], start=False, stop=False)
    return pe.matmul(out, w[1], x[0], start=False, stop=stop)


def program(nc, t, out):
    with ExitStack() as outer:
        def keep(name, shape, dt=F32):
            return outer.enter_context(nc.sbuf_tensor(name, shape, dt))

        ps = outer.enter_context(nc.psum_tensor("psum", [P, 8, BANK], F32))
        mem = {
            "x": keep("x_residual", [P, NT, D]),
            "ident": keep("ident", [P, P]),
            "mod0": keep("mod0", [P, 12, NB]),
            "mod1": keep("mod1", [P, 12, NB]),
            "neg_half": keep("neg_half", [P, TT]),
            "eps_col": keep("eps_col", [P, 1]),
            "silu_c1": keep("silu_c1", [P, DK, NB]),
        }
        modulation_stage(nc, t, ps, mem)
        mixer_stage(nc, t, ps, mem)
        recurrent_stage(nc, t, ps, mem)
        attention_stage(nc, t, ps, mem)
        zero_semaphores(nc)
        moe_stage(nc, t, ps, mem, out)



def zero_semaphores(nc):
    used = sorted(nc.released_uncleared_semaphores)
    assert used == list(range(used[0], used[-1] + 1))
    nc.gpsimd.sem_clear(range(used[0], used[-1] + 1))
    nc.all_engine_barrier()


def modulation_stage(nc, t, ps, mem):
    with ExitStack() as ctx:
        def sb(name, shape, dt=F32):
            return ctx.enter_context(nc.sbuf_tensor(name, shape, dt))

        def sem(name):
            return ctx.enter_context(nc.semaphore(name))

        cT = [sb(f"cT{l}", [P, DK, NB]) for l in range(2)]
        silu_c = [sb("silu_c0", [P, DK, NB]), mem["silu_c1"]]
        wmod = [sb(f"wmod{l}", [P, DK, 6 * D]) for l in range(2)]
        sign = sb("sign", [P, 2, DK, NB])
        mod = [mem["mod0"], mem["mod1"]]
        wmod_in, ident_in = [sem(f"md_wmod{l}") for l in range(2)], sem("md_ident")
        loaded, consts, silu_done, mod_done, raw, signed = (
            sem(n) for n in ("md_loaded", "md_consts", "md_silu", "md_product", "md_raw", "md_signed"))

        block = ctx.enter_context(nc.Block())

        @block.sync
        def _(sp):
            for l in range(2):
                sp.dma_start(cT[l][:, :, :], t[f"L{l}_cT"].rearrange("(k p) b -> p k b", p=P)).then_inc(loaded, 16)
            for l in range(2):
                sp.dma_start(wmod[l][:, :, :], t[f"L{l}_wmod"].rearrange("(k p) n -> p k n", p=P)
                             ).then_inc(wmod_in[l], 16)
            sp.dma_start(mem["ident"][:, :], t["ident"]).then_inc(ident_in, 16)
            sp.wait_ge(ident_in, 16)

        @block.scalar
        def _(act):
            act.wait_ge(loaded, 2 * 16)
            for l in range(2):
                act.activation(silu_c[l][:, :, :], cT[l][:, :, :], ACT.Silu).then_inc(silu_done, 1)

        @block.tensor
        def _(pe):
            for l in range(2):
                pe.wait_ge(silu_done, l + 1)
                pe.wait_ge(wmod_in[l], 16)
                for j in range(12):
                    for k in range(DK):
                        last = pe.matmul(ps[:, l, j * NB:(j + 1) * NB], wmod[l][:, k, j * P:(j + 1) * P],
                                         silu_c[l][:, k, :], start=(k == 0), stop=(k == DK - 1))
                last.then_inc(mod_done, 1)

        @block.vector
        def _(dve):
            dve.memset(mem["neg_half"][:, :], -0.5).then_inc(consts, 1)
            dve.memset(mem["eps_col"][:, :], EPS).then_inc(consts, 1)
            for l in range(2):
                table = mod[l]
                dve.wait_ge(mod_done, l + 1)
                dve.tensor_copy(table[:, :, :], ps[:, l, 0:12 * NB].rearrange("p (j b) -> p j b", b=NB)).then_inc(raw, 1)
                dve.wait_ge(raw, 3 * l + 1)
                for j in (SCALE_A, SCALE_B):
                    dve.tensor_scalar(table[:, j:j + 2, :], table[:, j:j + 2, :], 1.0, None, ALU.add).then_inc(raw, 1)
                for n, j in enumerate((GATE_A, GATE_B)):
                    gate = table[:, j:j + 2, :]
                    dve.tensor_scalar(sign[:, n], gate, 0.0, 2.0, ALU.is_ge, ALU.mult).then_inc(signed, 1)
                    dve.wait_ge(signed, 8 * l + 4 * n + 1)
                    dve.tensor_scalar(sign[:, n], sign[:, n], -1.0, None, ALU.add).then_inc(signed, 1)
                    dve.wait_ge(signed, 8 * l + 4 * n + 2)
                    dve.tensor_tensor(gate, gate, sign[:, n], ALU.mult).then_inc(signed, 1)
                    dve.wait_ge(signed, 8 * l + 4 * n + 3)
                    dve.scalar_tensor_tensor(gate, gate, 0.25, sign[:, n], ALU.max, ALU.mult).then_inc(signed, 1)
                dve.wait_ge(raw, 3 * l + 3)
                dve.wait_ge(signed, 8 * l + 8)


def mixer_weights(nc, t, ps, mem, w_in, w_conv, w_fc, w_out, w_comb, conv_b, neg_g, fc_bias, gate_bias, ones,
                  ones32, quads):
    with ExitStack() as ctx:
        def sb(name, shape, dt=F32):
            return ctx.enter_context(nc.sbuf_tensor("mw_" + name, shape, dt))

        def sem(name):
            return ctx.enter_context(nc.semaphore("mw_" + name))

        f_in = sb("in", [P, DK, 2 * INNER])
        f_conv = sb("conv", [P, IK * TAPS, P])
        f_fc = sb("fc", [P, IK, D])
        f_fcg = sb("fcg", [P, IK, D])
        f_out = sb("out", [P, IK, D])
        f_cproj = sb("cproj", [P, IK, D])
        f_comb = sb("comb", [P, DK, D])
        cols = sb("cols", [P, 4, IK])
        fc_b = sb("fc_b", [P, DK])
        out_b = sb("out_b", [P, DK])
        one = sb("one", [P, 1])
        x_in, big, small = sem("x"), sem("big"), sem("small")
        scaled, consts, folded, hi, comb = (sem(n) for n in ("scaled", "consts", "folded", "hi", "comb"))
        block = ctx.enter_context(nc.Block())

        @block.sync
        def _(sp):
            sp.dma_start(mem["x"][:, 0:TT, :], t["x"][0].rearrange("(n p) d -> p n d", p=P)).then_inc(x_in, 16)
            sp.dma_start(f_cproj[:, :, :], t["cproj_w"].rearrange("(k p) n -> p k n", p=P)).then_inc(small, 16)
            sp.dma_start(f_out[:, :, :], t["out_wT"].rearrange("(k p) n -> p k n", p=P)).then_inc(small, 16)
            sp.dma_start(f_fc[:, :, :], t["fc_wT"].rearrange("(k p) n -> p k n", p=P)).then_inc(small, 16)
            for n, name in enumerate(("ln_g", "ln_b", "cproj_b", "conv_b")):
                sp.dma_start(cols[:, n, :], t[name]).then_inc(small, 16)
            sp.dma_start(fc_b[:, :], t["fc_b"]).then_inc(small, 16)
            sp.dma_start(quads[:, :], t["quads"]).then_inc(small, 16)
            sp.dma_start(f_in[:, :, :], t["in_wT"].rearrange("(k p) n -> p k n", p=P)).then_inc(big, 16)
            sp.dma_start(f_conv[:, :, :], t["conv_blocks"].rearrange("n p m -> p n m")).then_inc(big, 16)
            sp.dma_start(mem["x"][:, TT:2 * TT, :], t["x"][1].rearrange("(n p) d -> p n d", p=P)).then_inc(x_in, 16)
            sp.wait_ge(x_in, 32)

        @block.vector
        def _(dve):
            dve.memset(one[:, :], 1.0).then_inc(consts, 1)
            dve.memset(ones32[:, :], 1.0 / INNER).then_inc(consts, 1)
            dve.wait_ge(consts, 2)
            dve.tensor_scalar(ones[:, :], one[:, 0:1].to_broadcast([P, P]), 1.0 / INNER, None, ALU.mult).then_inc(consts, 1)
            dve.wait_ge(small, 9 * 16)
            for k in range(IK):
                dve.tensor_scalar(f_fcg[:, k, :], f_fc[:, k, :], cols[:, 0, k:k + 1], None, ALU.mult).then_inc(scaled, 1)
            dve.tensor_copy(conv_b[:, :], cols[:, 3, :]).then_inc(consts, 1)
            dve.wait_ge(folded, 1)
            dve.tensor_scalar(neg_g[:, :], ps[:, 2, 0:DK], -1.0, None, ALU.mult).then_inc(comb, 1)
            dve.tensor_tensor(fc_bias[:, :], ps[:, 3, 0:DK], fc_b[:, :], ALU.add).then_inc(comb, 1)
            dve.tensor_copy(out_b[:, :], ps[:, 4, 0:DK]).then_inc(comb, 1)
            dve.tensor_copy(f_comb[:, :, :], ps[:, 0, :].rearrange("p (k n) -> p k n", k=DK)).then_inc(comb, 1)
            dve.wait_ge(comb, 3)
            for m in range(DK):
                dve.tensor_scalar(gate_bias[:, m, :], mem["mod0"][:, GATE_A + m, :], out_b[:, m:m + 1], None,
                                  ALU.mult).then_inc(comb, 1)
            for n, (f, w) in enumerate(((f_in, w_in), (f_conv, w_conv), (f_out, w_out), (f_fcg, w_fc),
                                        (f_comb, w_comb))):
                dve.wait_ge(hi, n + 1)
                dve.tensor_tensor(w[1][:, :, :], f[:, :, :], w[0][:, :, :].bitcast(F32), ALU.subtract).then_inc(consts, 1)
            dve.wait_ge(consts, 9)
            dve.wait_ge(comb, 6)

        @block.scalar
        def _(act):
            for n, (f, w) in enumerate(((f_in, w_in), (f_conv, w_conv), (f_out, w_out), (f_fcg, w_fc),
                                        (f_comb, w_comb))):
                if n < 2:
                    act.wait_ge(big, 32)
                elif n == 2:
                    act.wait_ge(small, 9 * 16)
                elif n == 3:
                    act.wait_ge(scaled, IK)
                else:
                    act.wait_ge(comb, 4)
                act.activation(w[0][:, :, :], f[:, :, :], ACT.Copy).then_inc(hi, 1)

        @block.tensor
        def _(pe):
            pe.wait_ge(small, 9 * 16)
            for m in range(DK):
                for k in range(IK):
                    pe.matmul(ps[:, 0, m * D:(m + 1) * D], f_cproj[:, k, m * P:(m + 1) * P], f_out[:, k, :],
                              start=(k == 0), stop=(k == IK - 1))
            pe.wait_ge(scaled, IK)
            pe.wait_ge(consts, 3)
            for bank, w, col in ((2, f_fcg, None), (3, f_fc, 1), (4, f_out, 2)):
                for m in range(DK):
                    for k in range(IK):
                        last = pe.matmul(ps[:, bank, m:m + 1], w[:, k, m * P:(m + 1) * P],
                                         one[:, :] if col is None else cols[:, col, k:k + 1],
                                         start=(k == 0), stop=(k == IK - 1))
            last.then_inc(folded, 1)


def mixer_stage(nc, t, ps, mem):
    x, ident, mod = mem["x"], mem["ident"], mem["mod0"]
    with ExitStack() as ctx:
        def sb(name, shape, dt=F32):
            return ctx.enter_context(nc.sbuf_tensor(name, shape, dt))

        def pair(name, shape):
            return sb(name + "_hi", shape, F32R), sb(name + "_lo", shape, F32R)

        def signal(name, per=1, before=0):
            return Signal(ctx, nc, "mx_" + name, per, before)

        w_in = pair("w_in", [P, DK, 2 * INNER])
        w_conv = pair("w_conv", [P, IK * TAPS, P])
        w_fc = pair("w_fc", [P, IK, D])
        w_out = pair("w_out", [P, IK, D])
        w_comb = pair("w_comb", [P, DK, D])
        conv_b = sb("conv_b", [P, IK])
        neg_g = sb("neg_g", [P, DK])
        fc_bias = sb("fc_bias", [P, DK])
        gate_bias = sb("gate_bias", [P, DK, NB])
        ones = sb("ones", [P, P], F32R)
        ones32 = sb("ones32", [P, 32])
        quads = sb("quads", [P, P])
        mixer_weights(nc, t, ps, mem, w_in, w_conv, w_fc, w_out, w_comb, conv_b, neg_g, fc_bias, gate_bias,
                      ones, ones32, quads)

        stats = sb("stats", [P, TT, 6])
        moments = sb("moments", [P, TT, 2])
        var_eps = sb("var_eps", [P, TT])
        rstd = sb("rstd", [P, TT])
        xn = sb("xn", [P, TT, D])
        hT = sb("hT", [P, DK, T])
        hT_s = pair("hT", [P, DK, T])
        h_s = pair("h", [P, IK, TAPS - 1 + T])
        gate = sb("gate", [P, IK, T])
        y = sb("y", [P, IK, T])
        y_s = pair("y", [P, IK, T])
        mean = sb("mean", [P, T])
        dev = y
        quad_sum = sb("quad_sum", [P, T])
        std = sb("std", [P, T])
        inv = std
        fc = hT
        fc_s = pair("fc", [P, DK, T])
        delta = sb("delta", [P, DK, T])

        (GATE0, OUTT, CONV, LNT, MEAN, FC, VQ, VB, OUT, H0) = (0, 4, 6, 10, 12, 13, 15, 16, 17, 19)

        def bank(slot):
            return ps[:, slot % 8, :]

        pads, x_rest = signal("pads"), signal("x_loaded")
        s_stat, s_mom, s_eps = signal("stat", TT), signal("moments", TT), signal("eps")
        s_pow, s_xn = signal("rstd"), signal("xn", TT)
        lnt, hTf, hTh, hTl = signal("ln_turned"), signal("hT_full", DK), signal("hT_hi", DK), signal("hT_lo", DK)
        hp, hh, hl = signal("h_product", IK), signal("h_hi", IK), signal("h_lo", IK)
        gp, gs = signal("gate_product", IK), signal("gate_silu", IK)
        cp, ys, yh, yl = signal("conv_product", IK), signal("y", IK), signal("y_hi", IK), signal("y_lo", IK)
        mp, ms, dv, sq = signal("mean_product"), signal("mean"), signal("dev", IK), signal("square", IK)
        vqp, vqs, vbp, sd, iv = signal("quad_product"), signal("quad"), signal("var"), signal("std"), signal("inv")
        fp, fc0, fc1 = signal("fc_product", DK), signal("fc_centred", DK), signal("fc_scaled", DK)
        fa, fh, fl = signal("fc_silu", DK), signal("fc_hi", DK), signal("fc_lo", DK)
        op, dl, ot, xs = signal("out_product", DK), signal("delta", DK), signal("out_turned", 2), signal("x_added", 2)

        block = ctx.enter_context(nc.Block())

        @block.sync
        def _(sp):
            for b in range(2, NB):
                sp.dma_start(x[:, b * TT:(b + 1) * TT, :],
                             t["x"][b].rearrange("(n p) d -> p n d", p=P)).then_inc(x_rest.sem, 16)

        def pe_turn_ln(pe, i):
            pe.wait_ge(*s_xn(i, TT))
            for f in range(DK):
                for n in range(TT):
                    last = pe.transpose(bank(LNT + f)[:, n * P:(n + 1) * P], xn[:, n, f * P:(f + 1) * P], ident[:, :])
            last.then_inc(lnt.sem, 1)

        def pe_h(pe, i, first):
            pe.wait_ge(*hTl(i, DK))
            for m in range(IK):
                if not first:
                    pe.wait_ge(*(hTf(i, 2), ms(i - 1, 1), fc0(i - 1, 1), fc0(i - 1, 2))[m])
                elif m == 0:
                    pe.wait_ge(*hTf(i, 2))
                for k in range(DK):
                    last = product3(pe, bank(H0 + m), [w[:, k, m * P:(m + 1) * P] for w in w_in],
                                    [h[:, k, :] for h in hT_s], k == 0, k == DK - 1)
                last.then_inc(hp.sem, 1)

        def pe_gate(pe, m):
            for k in range(DK):
                last = product3(pe, bank(GATE0 + m), [w[:, k, INNER + m * P:INNER + (m + 1) * P] for w in w_in],
                                [h[:, k, :] for h in hT_s], k == 0, k == DK - 1)
            last.then_inc(gp.sem, 1)

        def body(pe, i, first, last_batch):
            for m in range(1, IK):
                if m == 3:
                    pe.wait_ge(*hl(i, 1))
                elif not first:
                    pe.wait_ge(*dl(i - 1, m))
                pe_gate(pe, m)
            if not first:
                pe.wait_ge(*hl(i, 3))
                pe_turn_out(pe, i - 1)
            pe.wait_ge(*hl(i, 4))
            for m in range(IK):
                if m == 1 and not first:
                    pe.wait_ge(*vqs(i - 1, 1))
                if m >= 2:
                    pe.wait_ge(*gs(i, m - 1))
                for k in range(TAPS):
                    last = product3(pe, bank(CONV + m), [w[:, m * TAPS + k, :] for w in w_conv],
                                    [h[:, m, k:k + T] for h in h_s], k == 0, k == TAPS - 1)
                last.then_inc(cp.sem, 1)
            if not last_batch:
                pe.wait_ge(*gs(i, 4))
                pe_turn_ln(pe, i + 1)
            if not first:
                pe.wait_ge(*xs(i - 1, 2))
            for k in range(IK):
                pe.wait_ge(*yl(i, k + 1))
                for n, part in enumerate(y_s):
                    last = pe.matmul(bank(MEAN), ones[:, :], part[:, k, :], start=(k == 0 and n == 0),
                                     stop=(k == IK - 1 and n == 1))
            last.then_inc(mp.sem, 1)
            for m in range(DK):
                for k in range(IK):
                    last = product3(pe, bank(FC + m), [w[:, k, m * P:(m + 1) * P] for w in w_fc],
                                    [h[:, k, :] for h in y_s], k == 0, k == IK - 1)
                last.then_inc(fp.sem, 1)
            for m in range(DK):
                for k in range(IK):
                    if m == 0 and k == 2:
                        pe.wait_ge(*sq(i, 4))
                        for q in range(IK):
                            last = pe.matmul(bank(VQ)[32 * q:32 * q + 32, :], ones32[:, :], dev[:, q, :],
                                             start=True, stop=True, tile_position=(0, 32 * q))
                        last.then_inc(vqp.sem, 1)
                    if m == 1 and k == 0:
                        pe.wait_ge(*vqs(i, 1))
                        pe.matmul(bank(VB), quads[:, :], quad_sum[:, :], start=True, stop=True).then_inc(vbp.sem, 1)
                        if not last_batch:
                            pe.wait_ge(*hTf(i + 1, 1))
                    product3(pe, bank(OUT + m), [w[:, k, m * P:(m + 1) * P] for w in w_out],
                             [h[:, k, :] for h in y_s], k == 0, False)
            if not last_batch:
                pe_h(pe, i + 1, False)
                pe.wait_ge(*sd(i, 1))
                pe_gate(pe, 0)
            pe.wait_ge(*fl(i, 2))
            for m in range(DK):
                for k in range(DK):
                    last = product3(pe, bank(OUT + m), [w[:, k, m * P:(m + 1) * P] for w in w_comb],
                                    [h[:, k, :] for h in fc_s], False, k == DK - 1)
                last.then_inc(op.sem, 1)

        def pe_turn_out(pe, i):
            pe.wait_ge(*dl(i, 2))
            for n in range(TT):
                for f in range(DK):
                    last = pe.transpose(bank(OUTT + n // 2)[:, (n % 2) * D + f * P:(n % 2) * D + (f + 1) * P],
                                        delta[:, f, n * P:(n + 1) * P], ident[:, :])
                if n % 2:
                    last.then_inc(ot.sem, 1)

        @block.tensor
        def _(pe):
            pe_turn_ln(pe, 0)
            pe_h(pe, 0, True)
            pe_gate(pe, 0)
            body(pe, 0, True, False)
            with pe.Fori(1, NB - 1) as i:
                body(pe, i, False, False)
            body(pe, NB - 1, False, True)
            pe_turn_out(pe, NB - 1)

        def dve_stats(dve, i):
            for n in range(TT):
                tile = x[:, bass.ds(i * TT + n, 1), :].rearrange("p a d -> p (a d)")
                dve.bn_stats(stats[:, n, :], tile).then_inc(s_stat.sem, 1)
            for n in range(TT):
                dve.wait_ge(*s_stat(i, n + 1))
                dve.nop(nofuse=True)
                dve.bn_aggr(moments[:, n, :], stats[:, n, :]).then_inc(s_mom.sem, 1)
            dve.wait_ge(*s_mom(i, TT))
            dve.tensor_scalar(var_eps[:, :], moments[:, :, 1], EPS, None, ALU.add).then_inc(s_eps.sem, 1)

        def dve_norm(dve, i, first):
            if not first:
                dve.wait_ge(*lnt(i - 1, 1))
            dve.wait_ge(*s_pow(i, 1))
            for n in range(TT):
                tile = x[:, bass.ds(i * TT + n, 1), :].rearrange("p a d -> p (a d)")
                dve.tensor_scalar(xn[:, n, :], tile, moments[:, n, 0:1], rstd[:, n:n + 1],
                                  ALU.subtract, ALU.mult).then_inc(s_xn.sem, 1)

        def dve_hT_lo(dve, i, first):
            for f in range(DK):
                dve.wait_ge(*hTh(i, f + 1))
                dve.tensor_tensor(hT_s[1][:, f, :], hT[:, f, :], hT_s[0][:, f, :].bitcast(F32),
                                  ALU.subtract).then_inc(hTl.sem, 1)

        def dve_h_lo(dve, i, first):
            for m in range(IK):
                dve.wait_ge(*hh(i, m + 1))
                dve.tensor_tensor(h_s[1][:, m, TAPS - 1:], bank(H0 + m), h_s[0][:, m, TAPS - 1:].bitcast(F32),
                                  ALU.subtract).then_inc(hl.sem, 1)

        def dve_add(dve, i):
            for n in range(2):
                dve.wait_ge(*ot(i, n + 1))
                tiles = x[:, bass.ds(i * TT + 2 * n, 2), :]
                dve.tensor_tensor(tiles, tiles, bank(OUTT + n).rearrange("p (a d) -> p a d", a=2),
                                  ALU.add).then_inc(xs.sem, 1)

        def dve_body(dve, i, first, last_batch):
            if not last_batch:
                dve_stats(dve, i + 1)
            if not first:
                dve_add(dve, i - 1)
            if not last_batch:
                dve_norm(dve, i + 1, False)
            for m in range(IK):
                if m == 0 and not first:
                    dve.wait_ge(*op(i - 1, DK))
                    dve.wait_ge(*sq(i - 1, IK))
                dve.wait_ge(*cp(i, m + 1))
                dve.wait_ge(*gs(i, m + 1))
                dve.scalar_tensor_tensor(y[:, m, :], bank(CONV + m), conv_b[:, m:m + 1], gate[:, m, :],
                                         ALU.add, ALU.mult).then_inc(ys.sem, 1)
                if m:
                    dve.wait_ge(*yh(i, m))
                    dve.tensor_tensor(y_s[1][:, m - 1, :], y[:, m - 1, :], y_s[0][:, m - 1, :].bitcast(F32),
                                      ALU.subtract).then_inc(yl.sem, 1)
            dve.wait_ge(*yh(i, IK))
            dve.tensor_tensor(y_s[1][:, IK - 1, :], y[:, IK - 1, :], y_s[0][:, IK - 1, :].bitcast(F32),
                              ALU.subtract).then_inc(yl.sem, 1)
            if not last_batch:
                dve_hT_lo(dve, i + 1, False)
            for m in range(DK):
                dve.wait_ge(*fp(i, m + 1))
                dve.wait_ge(*ms(i, 1))
                if m == 0 and not last_batch:
                    dve.wait_ge(*hTl(i + 1, DK))
                dve.scalar_tensor_tensor(fc[:, m, :], mean[:, :], neg_g[:, m:m + 1], bank(FC + m),
                                         ALU.mult, ALU.add).then_inc(fc0.sem, 1)
            dve.wait_ge(*sd(i, 1))
            dve.reciprocal(inv[:, :], std[:, :]).then_inc(iv.sem, 1)
            for m in range(DK):
                dve.wait_ge(*iv(i, 1))
                dve.wait_ge(*fc0(i, m + 1))
                dve.tensor_tensor(fc[:, m, :], fc[:, m, :], inv[:, :], ALU.mult).then_inc(fc1.sem, 1)
            if not last_batch:
                dve_h_lo(dve, i + 1, False)
            for m in range(DK):
                dve.wait_ge(*fh(i, m + 1))
                dve.tensor_tensor(fc_s[1][:, m, :], fc[:, m, :], fc_s[0][:, m, :].bitcast(F32),
                                  ALU.subtract).then_inc(fl.sem, 1)

        @block.vector
        def _(dve):
            for part in h_s:
                dve.memset(part[:, :, 0:TAPS - 1].bitcast(U32), 0).then_inc(pads.sem, 1)
            dve_stats(dve, 0)
            dve_norm(dve, 0, True)
            dve_hT_lo(dve, 0, True)
            dve_h_lo(dve, 0, True)
            dve_body(dve, 0, True, False)
            dve.wait_ge(x_rest.sem, 16 * (NB - 2))
            with dve.Fori(1, NB - 1) as i:
                dve_body(dve, i, False, False)
            dve_body(dve, NB - 1, False, True)
            dve_add(dve, NB - 1)
            dve.wait_ge(*xs(NB - 1, 2))

        def pool_rstd(pool, i):
            pool.wait_ge(*s_eps(i, 1))
            pool.tensor_tensor(rstd[:, :], var_eps[:, :], mem["neg_half"][:, :], ALU.pow).then_inc(s_pow.sem, 1)

        def pool_body(pool, i, last_batch):
            if not last_batch:
                pool_rstd(pool, i + 1)
            for m in range(IK):
                if m == 0:
                    pool.wait_ge(*ms(i, 1))
                pool.tensor_tensor(dev[:, m, :], y[:, m, :], mean[:, :], ALU.subtract).then_inc(dv.sem, 1)

        @block.gpsimd
        def _(pool):
            pool_rstd(pool, 0)
            with pool.Fori(0, NB - 1) as i:
                pool_body(pool, i, False)
            pool_body(pool, NB - 1, True)

        def act_hT(act, i, first):
            for f in range(DK):
                if f == 0:
                    act.wait_ge(*lnt(i, 1))
                    act.nop(nofuse=True)
                act.activation(hT[:, f, :], bank(LNT + f), ACT.Identity,
                               bias=mod[:, SHIFT_A + f, bass.ds(i, 1)],
                               scale=mod[:, SCALE_A + f, bass.ds(i, 1)]).then_inc(hTf.sem, 1)
            for f in range(DK):
                act.wait_ge(*hTf(i, f + 1))
                act.activation(hT_s[0][:, f, :], hT[:, f, :], ACT.Copy).then_inc(hTh.sem, 1)

        def act_h_hi(act, i, first):
            for m in range(IK):
                if not first and m == 0:
                    act.wait_ge(*cp(i - 1, IK))
                act.wait_ge(*hp(i, m + 1))
                act.activation(h_s[0][:, m, TAPS - 1:], bank(H0 + m), ACT.Copy).then_inc(hh.sem, 1)

        def act_body(act, i, first, last_batch):
            for m in range(IK):
                if m == 0 and not first:
                    act.wait_ge(*ys(i - 1, IK))
                act.wait_ge(*gp(i, m + 1))
                act.activation(gate[:, m, :], bank(GATE0 + m), ACT.Silu).then_inc(gs.sem, 1)
            for m in range(IK):
                act.wait_ge(*ys(i, m + 1))
                act.activation(y_s[0][:, m, :], y[:, m, :], ACT.Copy).then_inc(yh.sem, 1)
            if not last_batch:
                act_hT(act, i + 1, False)
            act.wait_ge(*mp(i, 1))
            act.activation(mean[:, :], bank(MEAN), ACT.Copy).then_inc(ms.sem, 1)
            for m in range(IK):
                act.wait_ge(*dv(i, m + 1))
                act.activation(dev[:, m, :], dev[:, m, :], ACT.Square).then_inc(sq.sem, 1)
            act.wait_ge(*vqp(i, 1))
            act.activation(quad_sum[:, :], bank(VQ), ACT.Copy).then_inc(vqs.sem, 1)
            act.wait_ge(*vbp(i, 1))
            act.activation(std[:, :], bank(VB), ACT.Sqrt, bias=mem["eps_col"][:, 0:1]).then_inc(sd.sem, 1)
            for m in range(DK):
                act.wait_ge(*fc1(i, m + 1))
                act.activation(fc[:, m, :], fc[:, m, :], ACT.Silu, bias=fc_bias[:, m:m + 1]).then_inc(fa.sem, 1)
            for m in range(DK):
                if m == 0 and not first:
                    act.wait_ge(*op(i - 1, DK))
                act.wait_ge(*fa(i, m + 1))
                act.activation(fc_s[0][:, m, :], fc[:, m, :], ACT.Copy).then_inc(fh.sem, 1)
            if not last_batch:
                act_h_hi(act, i + 1, False)
            for m in range(DK):
                act.wait_ge(*op(i, m + 1))
                act.nop(nofuse=True)
                act.activation(delta[:, m, :], bank(OUT + m), ACT.Identity,
                               bias=gate_bias[:, m, bass.ds(i, 1)],
                               scale=mod[:, GATE_A + m, bass.ds(i, 1)]).then_inc(dl.sem, 1)

        @block.scalar
        def _(act):
            act_hT(act, 0, True)
            act_h_hi(act, 0, True)
            act_body(act, 0, True, False)
            with act.Fori(1, NB - 1) as i:
                act_body(act, i, False, False)
            act_body(act, NB - 1, False, True)



def recurrent_stage(nc, t, ps, mem):
    x, ident, mod = mem["x"], mem["ident"], mem["mod0"]
    STEPS = NB
    with ExitStack() as ctx:
        def sb(name, shape, dt=F32):
            return ctx.enter_context(nc.sbuf_tensor("rc_" + name, shape, dt))

        def pair(name, shape):
            return sb(name + "_hi", shape, F32R), sb(name + "_lo", shape, F32R)

        def signal(name, per=1, before=0):
            return Signal(ctx, nc, "rc_" + name, per, before)

        out_x = sb("out_x", [P, DK, STEPS * T])
        out_c = sb("out_c", [P, DK, T])
        names = ("wf", "wi", "wc", "wo", "uf", "ui", "uc", "uo")
        w = dict(zip(names, (pair(n, [P, DK, D]) for n in names)))
        bias = sb("bias", [P, 4, DK])
        c = sb("c", [P, DK, T])

        def signal(name, per=1, before=0):
            return Signal(ctx, nc, "rc_" + name, per, before)

        with ExitStack() as ctx_w:
            full = [ctx_w.enter_context(nc.sbuf_tensor(f"rc_full{n}", [P, DK, D], F32)) for n in range(4)]
            in_c = ctx_w.enter_context(nc.sbuf_tensor("rc_in_c", [P, DK], F32))
            loaded = [ctx_w.enter_context(nc.semaphore(f"rc_loaded{n}")) for n in range(len(names))]
            small, hi, lo, start = (ctx_w.enter_context(nc.semaphore("rcw_" + n)) for n in ("small", "hi", "lo", "start"))
            with nc.Block() as block:
                @block.sync
                def _(sp):
                    for n, name in enumerate(names):
                        if n >= len(full):
                            sp.wait_ge(lo, n - len(full) + 1)
                        sp.dma_start(full[n % len(full)][:, :, :],
                                     t[name + "T"].rearrange("(k p) n -> p k n", p=P)).then_inc(loaded[n], 16)
                        if n == 0:
                            for j, b in enumerate(("bf", "bi", "bc", "bo")):
                                sp.dma_start(bias[:, j, :], t[b]).then_inc(small, 16)
                            sp.dma_start(in_c[:, :], t["in_c"]).then_inc(small, 16)
                    sp.wait_ge(small, 5 * 16)

                @block.scalar
                def _(act):
                    for n, name in enumerate(names):
                        act.wait_ge(loaded[n], 16)
                        act.activation(w[name][0][:, :, :], full[n % len(full)][:, :, :], ACT.Copy).then_inc(hi, 1)

                @block.vector
                def _(dve):
                    dve.wait_ge(small, 5 * 16)
                    dve.tensor_copy(c[:, :, :], in_c[:, :].unsqueeze(2).to_broadcast([P, DK, T])).then_inc(start, 1)
                    for n, name in enumerate(names):
                        dve.wait_ge(hi, n + 1)
                        dve.tensor_tensor(w[name][1][:, :, :], full[n % len(full)][:, :, :],
                                          w[name][0][:, :, :].bitcast(F32), ALU.subtract).then_inc(lo, 1)
                    dve.wait_ge(start, 1)
                    dve.wait_ge(lo, len(names))

        with ExitStack() as ctx:
            stats = sb2(ctx, nc, "rc_stats", [P, TT, 6])
            moments = sb2(ctx, nc, "rc_moments", [P, TT, 2])
            var_eps = sb2(ctx, nc, "rc_var_eps", [P, TT])
            rstd = sb2(ctx, nc, "rc_rstd", [P, TT])
            xn = sb2(ctx, nc, "rc_xn", [P, TT, D])
            hT = sb2(ctx, nc, "rc_hT", [P, DK, T])
            hT_s = [sb2(ctx, nc, f"rc_hT_{n}", [P, DK, T], F32R) for n in ("hi", "lo")]
            c_s = [sb2(ctx, nc, f"rc_c_{n}", [P, DK, T], F32R) for n in ("hi", "lo")]
            gates = [sb2(ctx, nc, f"rc_gate_{n}", [P, DK, T]) for n in ("forget", "input", "new")]
            F, I, G = 0, 1, 2

            def sig(name, per=1, before=0):
                return Signal(ctx, nc, "rc_" + name, per, before)

            s_stat, s_mom, s_eps = sig("stat", TT), sig("moments", TT), sig("eps")
            s_pow, s_xn = sig("rstd"), sig("xn", TT)
            lnt, hTf, hTh, hTl = sig("ln_turned"), sig("hT_full", DK), sig("hT_hi", DK), sig("hT_lo", DK)
            up, ga = sig("gate_product", 3 * DK), sig("gate", 3 * DK)
            keepc, new, cu = sig("kept", DK), sig("added", DK), sig("c", DK)
            ch, cl = sig("c_hi", DK, DK), sig("c_lo", DK, DK)
            op, oe = sig("out_product", DK), sig("out_kept", DK)
            cop, coe = sig("outc_product"), sig("outc_kept")

            def bank(slot):
                return ps[:, slot, :]

            SIDE = 6
            LEFT = (("wi", "ui"), ("wc", "uc"), ("wf", "uf"))
            ORDER = (I, G, F)

            block = ctx.enter_context(nc.Block())

            def pe_turn(pe, i, first):
                pe.wait_ge(*s_xn(i, TT))
                if not first:
                    pe.wait_ge(*oe(i - 1, DK))
                for f in range(DK):
                    for n in range(TT):
                        last = pe.transpose(bank(SIDE + f)[:, n * P:(n + 1) * P], xn[:, n, f * P:(f + 1) * P],
                                            ident[:, :])
                last.then_inc(lnt.sem, 1)

            def pe_inputs(pe, i, first):
                pe.wait_ge(*hTl(i, DK))
                for m in range(DK):
                    for k in range(DK):
                        last = product3(pe, bank(SIDE + m), [v[:, k, m * P:(m + 1) * P] for v in w["wo"]],
                                        [h[:, k, :] for h in hT_s], k == 0, k == DK - 1)
                    last.then_inc(op.sem, 1)
                for m in range(DK):
                    for g in range(3):
                        if not first:
                            pe.wait_ge(*ga(i - 1, 3 * m + g + 1))
                        for k in range(DK):
                            product3(pe, bank(3 * m + g), [v[:, k, m * P:(m + 1) * P] for v in w[LEFT[g][0]]],
                                     [h[:, k, :] for h in hT_s], k == 0, False)

            def pe_step(pe, i, last_step):
                if not last_step:
                    pe_turn(pe, i + 1, False)
                pe.wait_ge(*cl(i - 1, DK))
                for m in range(DK):
                    for g in range(3):
                        for k in range(DK):
                            last = product3(pe, bank(3 * m + g), [v[:, k, m * P:(m + 1) * P] for v in w[LEFT[g][1]]],
                                            [h[:, k, :] for h in c_s], False, k == DK - 1)
                        last.then_inc(up.sem, 1)
                if not last_step:
                    pe_inputs(pe, i + 1, False)

            @block.tensor
            def _(pe):
                pe_turn(pe, 0, True)
                pe_inputs(pe, 0, True)
                with pe.Fori(0, STEPS - 1) as i:
                    pe_step(pe, i, False)
                pe_step(pe, STEPS - 1, True)
                pe.wait_ge(*cl(STEPS - 1, DK))
                pe.wait_ge(*oe(STEPS - 1, DK))
                for m in range(DK):
                    for k in range(DK):
                        last = product3(pe, bank(SIDE + m), [v[:, k, m * P:(m + 1) * P] for v in w["uo"]],
                                        [h[:, k, :] for h in c_s], k == 0, k == DK - 1)
                last.then_inc(cop.sem, 1)

            def dve_layer_norm(dve, i, first):
                for n in range(TT):
                    tile = x[:, bass.ds(i * TT + n, 1), :].rearrange("p a d -> p (a d)")
                    dve.bn_stats(stats[:, n, :], tile).then_inc(s_stat.sem, 1)
                for n in range(TT):
                    dve.wait_ge(*s_stat(i, n + 1))
                    dve.nop(nofuse=True)
                    dve.bn_aggr(moments[:, n, :], stats[:, n, :]).then_inc(s_mom.sem, 1)
                dve.wait_ge(*s_mom(i, TT))
                dve.tensor_scalar(var_eps[:, :], moments[:, :, 1], EPS, None, ALU.add).then_inc(s_eps.sem, 1)
                if not first:
                    dve.wait_ge(*lnt(i - 1, 1))
                dve.wait_ge(*s_pow(i, 1))
                for n in range(TT):
                    tile = x[:, bass.ds(i * TT + n, 1), :].rearrange("p a d -> p (a d)")
                    dve.tensor_scalar(xn[:, n, :], tile, moments[:, n, 0:1], rstd[:, n:n + 1],
                                      ALU.subtract, ALU.mult).then_inc(s_xn.sem, 1)

            def dve_hT_lo(dve, i):
                for f in range(DK):
                    dve.wait_ge(*hTh(i, f + 1))
                    dve.tensor_tensor(hT_s[1][:, f, :], hT[:, f, :], hT_s[0][:, f, :].bitcast(F32),
                                      ALU.subtract).then_inc(hTl.sem, 1)

            def dve_c_lo(dve, i):
                for m in range(DK):
                    dve.wait_ge(*ch(i, m + 1))
                    dve.tensor_tensor(c_s[1][:, m, :], c[:, m, :], c_s[0][:, m, :].bitcast(F32),
                                      ALU.subtract).then_inc(cl.sem, 1)

            def dve_step(dve, i, last_step):
                if not last_step:
                    dve_hT_lo(dve, i + 1)
                for m in range(DK):
                    dve.wait_ge(*ga(i, 3 * m + 3))
                    dve.tensor_tensor(gates[F][:, m, :], gates[F][:, m, :], c[:, m, :], ALU.mult).then_inc(keepc.sem, 1)
                    dve.wait_ge(*keepc(i, m + 1))
                    dve.wait_ge(*new(i, m + 1))
                    dve.wait_ge(*cl(i - 1, m + 1))
                    dve.tensor_tensor(c[:, m, :], gates[F][:, m, :], gates[I][:, m, :], ALU.add).then_inc(cu.sem, 1)
                dve_c_lo(dve, i)

            @block.vector
            def _(dve):
                dve_layer_norm(dve, 0, True)
                dve_c_lo(dve, -1)
                dve_hT_lo(dve, 0)
                dve_layer_norm(dve, 1, False)
                with dve.Fori(0, STEPS - 2) as i:
                    dve_step(dve, i, False)
                    dve_layer_norm(dve, i + 2, False)
                dve_step(dve, STEPS - 2, False)
                dve_step(dve, STEPS - 1, True)

            def pool_rstd(pool, i):
                pool.wait_ge(*s_eps(i, 1))
                pool.tensor_tensor(rstd[:, :], var_eps[:, :], mem["neg_half"][:, :], ALU.pow).then_inc(s_pow.sem, 1)

            def pool_new(pool, i):
                for m in range(DK):
                    pool.wait_ge(*ga(i, 3 * m + 2))
                    pool.tensor_tensor(gates[I][:, m, :], gates[I][:, m, :], gates[G][:, m, :],
                                       ALU.mult).then_inc(new.sem, 1)

            @block.gpsimd
            def _(pool):
                pool_rstd(pool, 0)
                pool_rstd(pool, 1)
                with pool.Fori(0, STEPS - 2) as i:
                    pool_new(pool, i)
                    pool_rstd(pool, i + 2)
                pool_new(pool, STEPS - 2)
                pool_new(pool, STEPS - 1)

            def act_hT(act, i):
                act.wait_ge(*lnt(i, 1))
                act.nop(nofuse=True)
                for f in range(DK):
                    act.activation(hT[:, f, :], bank(SIDE + f), ACT.Identity,
                                   bias=mod[:, SHIFT_B + f, bass.ds(i, 1)],
                                   scale=mod[:, SCALE_B + f, bass.ds(i, 1)]).then_inc(hTf.sem, 1)
                for f in range(DK):
                    act.wait_ge(*hTf(i, f + 1))
                    act.activation(hT_s[0][:, f, :], hT[:, f, :], ACT.Copy).then_inc(hTh.sem, 1)

            def act_out(act, i):
                for m in range(DK):
                    act.wait_ge(*op(i, m + 1))
                    act.nop(nofuse=True)
                    act.activation(out_x[:, m, bass.ds(i * T, T)], bank(SIDE + m), ACT.Identity,
                                   bias=bias[:, 3, m:m + 1]).then_inc(oe.sem, 1)

            def act_c_hi(act, i):
                for m in range(DK):
                    if not (isinstance(i, int) and i < 0):
                        act.wait_ge(*cu(i, m + 1))
                    act.activation(c_s[0][:, m, :], c[:, m, :], ACT.Copy).then_inc(ch.sem, 1)

            def act_step(act, i, last_step):
                if not last_step:
                    act_hT(act, i + 1)
                for m in range(DK):
                    for g in range(3):
                        act.wait_ge(*up(i, 3 * m + g + 1))
                        act.activation(gates[ORDER[g]][:, m, :], bank(3 * m + g),
                                       ACT.Tanh if ORDER[g] == G else ACT.Sigmoid,
                                       bias=bias[:, (1, 2, 0)[g], m:m + 1]).then_inc(ga.sem, 1)
                act_c_hi(act, i)
                if not last_step:
                    act_out(act, i + 1)

            @block.scalar
            def _(act):
                act_c_hi(act, -1)
                act_hT(act, 0)
                act_out(act, 0)
                with act.Fori(0, STEPS - 1) as i:
                    act_step(act, i, False)
                act_step(act, STEPS - 1, True)
                act.wait_ge(*cop(0, 1))
                act.activation(out_c[:, :, :], ps[:, SIDE:SIDE + 2, :], ACT.Copy).then_inc(coe.sem, 1)
                act.wait_ge(*coe(0, 1))

        with ExitStack() as ctx:
            z = [sb2(ctx, nc, f"rt_z{n}", [P, DK, T]) for n in range(2)]
            d = [sb2(ctx, nc, f"rt_d{n}", [P, DK, T]) for n in range(2)]
            zs, th, sc, tu, ad = (Signal(ctx, nc, "rt_" + n, 2) for n in ("sum", "tanh", "gated", "turned", "added"))
            block = ctx.enter_context(nc.Block())

            @block.gpsimd
            def _(pool):
                def step(i, u, first):
                    if not first:
                        pool.wait_ge(*th(i - 1, u + 1))
                    pool.tensor_tensor(z[u][:, :, :], out_x[:, :, bass.ds((2 * i + u) * T, T)], out_c[:, :, :],
                                       ALU.add).then_inc(zs.sem, 1)
                step(0, 0, True)
                step(0, 1, True)
                with pool.Fori(1, NB // 2) as i:
                    for u in range(2):
                        if u == 0:
                            pool.wait_ge(*th(i - 1, 1))
                        else:
                            pool.wait_ge(*th(i - 1, 2))
                        pool.nop(nofuse=True)
                        pool.tensor_tensor(z[u][:, :, :], out_x[:, :, bass.ds((2 * i + u) * T, T)], out_c[:, :, :],
                                           ALU.add).then_inc(zs.sem, 1)

            @block.scalar
            def _(act):
                def step(i, u, first):
                    act.wait_ge(*zs(i, u + 1))
                    if not first:
                        act.wait_ge(*tu(i - 1, u + 1))
                    act.activation(d[u][:, :, :], z[u][:, :, :], ACT.Tanh).then_inc(th.sem, 1)
                    act.wait_ge(*th(i, u + 1))
                    act.nop(nofuse=True)
                    for m in range(DK):
                        last = act.activation(d[u][:, m, :], d[u][:, m, :], ACT.Copy,
                                              scale=mod[:, GATE_B + m, bass.ds(2 * i + u, 1)])
                    last.then_inc(sc.sem, 1)
                for u in range(2):
                    step(0, u, True)
                with act.Fori(1, NB // 2) as i:
                    for u in range(2):
                        step(i, u, False)

            @block.tensor
            def _(pe):
                def step(i, u, first):
                    pe.wait_ge(*sc(i, u + 1))
                    if not first:
                        pe.wait_ge(*ad(i - 1, u + 1))
                    for n in range(TT):
                        for f in range(DK):
                            last = pe.transpose(ps[:, 2 * u + n // 2, (n % 2) * D + f * P:(n % 2) * D + (f + 1) * P],
                                                d[u][:, f, n * P:(n + 1) * P], ident[:, :])
                    last.then_inc(tu.sem, 1)
                for u in range(2):
                    step(0, u, True)
                with pe.Fori(1, NB // 2) as i:
                    for u in range(2):
                        step(i, u, False)

            @block.vector
            def _(dve):
                with dve.Fori(0, NB // 2) as i:
                    for u in range(2):
                        dve.wait_ge(*tu(i, u + 1))
                        tiles = x[:, bass.ds((2 * i + u) * TT, TT), :]
                        dve.tensor_tensor(tiles, tiles, ps[:, 2 * u:2 * u + 2, :].rearrange(
                            "p k (a d) -> p (k a) d", a=2), ALU.add).then_inc(ad.sem, 1)
                dve.wait_ge(*ad(NB // 2 - 1, 2))


def sb2(ctx, nc, name, shape, dt=F32):
    return ctx.enter_context(nc.sbuf_tensor(name, shape, dt))



HEADS = 16
HD = 16
GROUP = 4
NG = HEADS // GROUP
AHEAD = 7
ATT_SCALE = HD ** -0.5
Q_PARTS = (0, 0, 0, 1, 1, 2)
K_PARTS = (0, 1, 2, 0, 1, 0)
LOADS = ((0, (0, 3), slice(0, 1)), (0, (3, 5), slice(1, 2)), (0, (5, 6), slice(2, 3)),
         (1, (0, 3), slice(0, 3)), (1, (3, 5), slice(0, 2)), (1, (5, 6), slice(0, 1)))
N_STORES = 2 * 3 * 2
STACK = len(Q_PARTS) * HD


def attention_weights(nc, t, ps, mem, wq, wk, wv, wo, ident_b, mask_q, mask_k):
    with ExitStack() as ctx:
        def sb(name, shape, dt=F32):
            return ctx.enter_context(nc.sbuf_tensor("aw_" + name, shape, dt))

        def sem(name):
            return ctx.enter_context(nc.semaphore("aw_" + name))

        f_qT, f_q = sb("qT", [P, DK, D]), sb("q", [P, DK, D])
        f_k, f_v, f_o = sb("k", [P, DK, D]), sb("v", [P, DK, D]), sb("o", [P, DK, D])
        dirs, sdirs, scales = sb("dirs", [HEADS, D]), sb("sdirs", [HEADS, D]), sb("scales", [HEADS, 1])
        form = sb("form", [P, DK, D])
        masks = sb("masks", [P, 2, P])
        small, big, fold, prod, hi, lo, const = (sem(n) for n in ("small", "big", "fold", "prod", "hi", "lo", "const"))
        block = ctx.enter_context(nc.Block())

        @block.sync
        def _(sp):
            sp.dma_start(dirs[:, :], t["head_dirs"]).then_inc(small, 16)
            sp.dma_start(scales[:, :], t["head_scales"]).then_inc(small, 16)
            sp.dma_start(f_qT[:, :, :], t["wqT"].rearrange("(k p) n -> p k n", p=P)).then_inc(small, 16)
            for n, f in enumerate((f_k, f_v)):
                sp.dma_start(f[:, :, :], t["w_qkv"][:, (n + 1) * D:(n + 2) * D].rearrange(
                    "(k p) n -> p k n", p=P)).then_inc(big, 16)
            sp.dma_start(f_o[:, :, :], t["w_out1"].rearrange("(k p) n -> p k n", p=P)).then_inc(big, 16)
            sp.dma_start(masks[:, :, :], t["masks"].rearrange("n p m -> p n m")).then_inc(big, 16)

        @block.vector
        def _(dve):
            dve.wait_ge(small, 48)
            dve.tensor_scalar(sdirs[:, :], dirs[:, :], scales[:, 0:1], None, ALU.mult).then_inc(fold, 1)
            dve.wait_ge(prod, 1)
            dve.tensor_copy(form[:, :, :], ps[:, 0, :].rearrange("p (k n) -> p k n", k=DK)).then_inc(fold, 1)
            dve.wait_ge(fold, 2)
            for m in range(DK):
                d = form[:, m, m * P:(m + 1) * P]
                dve.scalar_tensor_tensor(d, mem["ident"][:, :], ATT_SCALE, d, ALU.mult, ALU.add).then_inc(fold, 1)
            dve.wait_ge(prod, 2)
            dve.tensor_copy(f_q[:, :, :], ps[:, 1, :].rearrange("p (k n) -> p k n", k=DK)).then_inc(fold, 1)
            dve.wait_ge(big, 64)
            dve.tensor_copy(ident_b[:, :], mem["ident"][:, :]).then_inc(const, 1)
            dve.tensor_copy(mask_q[:, :], masks[:, 0, :]).then_inc(const, 1)
            dve.tensor_copy(mask_k[:, :], masks[:, 1, :]).then_inc(const, 1)
            for n, (f, w) in enumerate(((f_q, wq), (f_k, wk), (f_v, wv), (f_o, wo))):
                dve.wait_ge(hi, n + 1)
                dve.tensor_tensor(w[1][:, :, :], f[:, :, :], w[0][:, :, :].bitcast(F32), ALU.subtract).then_inc(lo, 1)
            dve.wait_ge(lo, 4)
            dve.wait_ge(const, 3)

        @block.scalar
        def _(act):
            for n, (f, w) in enumerate(((f_q, wq), (f_k, wk), (f_v, wv), (f_o, wo))):
                if n == 0:
                    act.wait_ge(fold, 5)
                if n == 1:
                    act.wait_ge(big, 64)
                act.activation(w[0][:, :, :], f[:, :, :], ACT.Copy).then_inc(hi, 1)

        @block.tensor
        def _(pe):
            pe.wait_ge(fold, 1)
            for m in range(DK):
                last = pe.matmul(ps[:, 0, m * D:(m + 1) * D], dirs[:, m * P:(m + 1) * P], sdirs[:, :],
                                 start=True, stop=True)
            last.then_inc(prod, 1)
            pe.wait_ge(fold, 4)
            for m in range(DK):
                for k in range(DK):
                    last = pe.matmul(ps[:, 1, m * D:(m + 1) * D], f_qT[:, k, m * P:(m + 1) * P], form[:, k, :],
                                     start=(k == 0), stop=(k == DK - 1))
            last.then_inc(prod, 1)


def attention_stage(nc, t, ps, mem):
    x, ident, mod = mem["x"], mem["ident"], mem["mod1"]
    with ExitStack() as ctx:
        def sb(name, shape, dt=F32):
            return ctx.enter_context(nc.sbuf_tensor("at_" + name, shape, dt))

        def pair(name, shape):
            return sb(name + "_hi", shape, F32R), sb(name + "_lo", shape, F32R)

        def signal(name, per=1, before=0):
            return Signal(ctx, nc, "at_" + name, per, before)

        wq, wk, wv, wo = (pair(n, [P, DK, D]) for n in ("wq", "wk", "wv", "wo"))
        ident_b, mask_q, mask_k = (sb(n, [P, P], BF16) for n in ("ident_b", "mask_q", "mask_k"))
        attention_weights(nc, t, ps, mem, wq, wk, wv, wo, ident_b, mask_q, mask_k)

        parts_dram = nc.dram_tensor("qk_parts", (2, 3, HD, HEADS, T), BF16, kind="Internal").ap()
        q_stack = sb("q_stack", [P, HEADS, T], BF16)
        k_stack = sb("k_stack", [P, HEADS, T], BF16)
        probs = sb("probs", [P, GROUP + 1, 1280])
        values = sb("values", [P, TT, HEADS, 32])
        stats, moments = sb("stats", [P, TT, 6]), sb("moments", [P, TT, 2])
        var_eps, rstd = sb("var_eps", [P, TT]), sb("rstd", [P, TT])
        xn = sb("xn", [P, TT, D])
        hT = sb("hT", [P, DK, T])
        rest = hT
        hT_s = pair("hT", [P, DK, T])
        qk_parts = [sb(n, [P, 3, DK, T], BF16) for n in ("q_parts", "k_parts")]
        top = sb("top", [P, HEADS, TT])
        neg_top = sb("neg_top", [HEADS, 3, P], BF16)
        neg_rest = sb("neg_rest", [HEADS, P])
        oT = sb("oT", [P, T])
        recip = sb("recip", [P, TT, GROUP])
        o_tok = sb("o_tok", [P, TT, D])
        o_s = pair("o", [P, DK, T])
        delta = sb("delta", [P, DK, T])

        def bank(n):
            return ps[:, n, :]

        MAX0, SIDE_A, PV_BANK, SIDE_B = 3, 5, 6, 7
        MAX_TILES = (((3, 0),), ((2, 0), (0, 384)), ((1, 0),))

        def slot(h):
            return GROUP if h % (2 * GROUP) == GROUP else h % GROUP

        ST_PLACE = {0: (0, 0), 1: (1, 0), 3: (1, 384), 2: (2, 0)}
        P_COL = {0: 0, 1: 512, 3: 896, 2: 1024}

        const = signal("const")
        s_stat, s_mom, s_eps = signal("stat", TT), signal("moments", TT), signal("eps")
        s_pow, s_xn = signal("rstd"), signal("xn", TT)
        lnt, hTf, hTh, hTl = signal("ln_turned"), signal("hT_full", DK), signal("hT_hi", DK), signal("hT_lo", DK)
        vp, ve = signal("v_product", 2), signal("v_kept", 2)
        qp, q1, qr, q2, q3 = (signal(n, 4) for n in ("qk_product", "qk_part1", "qk_rest", "qk_part2", "qk_part3"))
        stored = signal("stored", 16 * N_STORES)
        loaded = [signal(f"loaded{g}", 16 * len(LOADS)) for g in range(NG)]
        mxp, mxr = signal("max_scores", 3 * HEADS), signal("max", 4 * HEADS)
        mtp, neg, row = signal("max_turned", NG), signal("neg_max", 4 * NG), [signal(f"max_row{g}", 48) for g in range(NG)]
        stp, ex = signal("scores", 3 * HEADS), signal("exp", 3 * HEADS)
        pv, oe, otp, rc, on = (signal(n, NG) for n in ("pv", "oT_kept", "oT_turned", "recip", "o_normal"))
        yp, yh, yl = signal("o_turned", DK), signal("o_hi", DK), signal("o_lo", DK)
        wp, dl, hp, xs = signal("out_product", DK), signal("delta", DK), signal("delta_turned", 2), signal("x_added", 2)

        block = ctx.enter_context(nc.Block())

        def pe_max(pe, b, h, f):
            if h % GROUP == 0 and f == 0:
                pe.wait_ge(*loaded[h // GROUP](b, loaded[0].per))
            n = 3 * h + f
            if n >= 2:
                pe.wait_ge(*mxr(b, 4 * ((n - 2) // 3) + (1, 3, 4)[(n - 2) % 3]))
            elif not (isinstance(b, int) and b == 0):
                pe.wait_ge(*mxr(b - 1, 4 * HEADS - 1 + n))
            for qt, col in MAX_TILES[f]:
                w = (qt + 1) * P
                out = bank(MAX0 + n % 2)[:, col:col + w]
                pe.matmul(out, q_stack[0:STACK, h, qt * P:(qt + 1) * P], k_stack[0:STACK, h, 0:w],
                          start=True, stop=True)
                last = pe.matmul(bank(MAX0 + n % 2)[:, col + w - P:col + w], ident_b[:, :], mask_q[:, :],
                                 start=False, stop=True, skip_group_check=True)
            last.then_inc(mxp.sem, 1)

        def pe_scores(pe, b, h, f, first):
            if h % GROUP == 0 and f == 0:
                pe.wait_ge(*row[h // GROUP](b, 48))
            if h:
                pe.wait_ge(*ex(b, 3 * (h - 1) + f + 1))
            elif not first:
                pe.wait_ge(*ex(b - 1, 3 * (HEADS - 1) + f + 1))
            for kt in ((0,), (1, 3), (2,))[f]:
                bk, col = ST_PLACE[kt]
                w = T - kt * P
                pe.matmul(bank(bk)[:, col:col + w], k_stack[0:STACK + 3, h, kt * P:(kt + 1) * P],
                          q_stack[0:STACK + 3, h, kt * P:T], start=True, stop=True)
                last = pe.matmul(bank(bk)[:, col:col + P], ident_b[:, :], mask_k[:, :],
                                 start=False, stop=True, skip_group_check=True)
            last.then_inc(stp.sem, 1)

        def pe_pv(pe, b, g):
            pe.wait_ge(*ex(b, 3 * GROUP * (g + 1)))
            if g == 0:
                pe.wait_ge(*ve(b, 2))
                if not (isinstance(b, int) and b == 0):
                    pe.wait_ge(*oe(b - 1, NG))
            else:
                pe.wait_ge(*oe(b, g))
            for kt in range(TT):
                for hh in range(GROUP):
                    w = T - kt * P
                    last = pe.matmul(bank(PV_BANK)[32 * hh:32 * hh + 32, kt * P:T], values[:, kt, GROUP * g + hh, :],
                                     probs[:, slot(GROUP * g + hh), P_COL[kt]:P_COL[kt] + w], start=(kt == 0), stop=(kt == TT - 1),
                                     tile_position=(0, 32 * hh), skip_group_check=True)
            last.then_inc(pv.sem, 1)

        def pe_values(pe, b):
            for n in range(2):
                for a in range(2):
                    for k in range(DK):
                        tile = slice((2 * n + a) * P, (2 * n + a + 1) * P)
                        last = product3(pe, bank((SIDE_A, SIDE_B)[n])[:, a * D:(a + 1) * D],
                                        [h[:, k, tile] for h in hT_s], [w[:, k, :] for w in wv], k == 0, k == DK - 1)
                last.then_inc(vp.sem, 1)

        def pe_turn_ln(pe, b):
            pe.wait_ge(*s_xn(b, TT))
            for f in range(DK):
                for n in range(TT):
                    last = pe.transpose(bank((SIDE_A, SIDE_B)[f])[:, n * P:(n + 1) * P], xn[:, n, f * P:(f + 1) * P],
                                        ident[:, :])
            last.then_inc(lnt.sem, 1)

        def pe_qk(pe, n):
            w, m = (wq, wk)[n // 2], n % 2
            for k in range(DK):
                last = product3(pe, bank((SIDE_A, SIDE_B)[m]), [v[:, k, m * P:(m + 1) * P] for v in w],
                                [h[:, k, :] for h in hT_s], k == 0, k == DK - 1)
            last.then_inc(qp.sem, 1)

        def pe_turn_max(pe, b, g):
            pe.wait_ge(*mxr(b, 4 * GROUP * (g + 1)))
            pe.transpose(bank(PV_BANK)[0:HEADS, 0:P], top[:, GROUP * g:GROUP * (g + 1), :].rearrange("p h q -> p (h q)"),
                         ident[:, :]).then_inc(mtp.sem, 1)

        def pe_turn_o(pe, b, g, side):
            pe.wait_ge(*oe(b, g + 1))
            for n in range(TT):
                last = pe.transpose(bank(side)[:, n * P:(n + 1) * P], oT[:, n * P:(n + 1) * P], ident[:, :])
            last.then_inc(otp.sem, 1)

        def pe_turn_tok(pe, b, f):
            pe.wait_ge(*on(b, NG))
            for n in range(TT):
                last = pe.transpose(bank((SIDE_A, SIDE_B)[f])[:, n * P:(n + 1) * P], o_tok[:, n, f * P:(f + 1) * P],
                                    ident[:, :])
            last.then_inc(yp.sem, 1)

        def pe_out(pe, b, m):
            pe.wait_ge(*yl(b, DK))
            for k in range(DK):
                last = product3(pe, bank((SIDE_A, SIDE_B)[m]), [v[:, k, m * P:(m + 1) * P] for v in wo],
                                [h[:, k, :] for h in o_s], k == 0, k == DK - 1)
            last.then_inc(wp.sem, 1)

        def pe_turn_delta(pe, b, n):
            pe.wait_ge(*dl(b, DK))
            for a in range(2):
                for f in range(DK):
                    tile = slice((2 * n + a) * P, (2 * n + a + 1) * P)
                    last = pe.transpose(bank(SIDE_B)[:, a * D + f * P:a * D + (f + 1) * P], delta[:, f, tile], ident[:, :])
            last.then_inc(hp.sem, 1)

        def pe_batch(pe, i, first, last):
            for h in range(HEADS):
                for f in range(3):
                    if f == 2 and h % GROUP == 0 and not (first and h == 0):
                        pe.wait_ge(*neg(i, 4 * (h // GROUP + 1)))
                        pe_pv(pe, *((i, h // GROUP - 1) if h else (i - 1, NG - 1)))
                    pe_scores(pe, i, h, f, first)
                    if h + AHEAD < HEADS:
                        pe_max(pe, i, h + AHEAD, f)
                    elif not last:
                        pe_max(pe, i + 1, h + AHEAD - HEADS, f)
                if h % GROUP == 1 and not (last and h + GROUP > HEADS):
                    g = h // GROUP
                    if g:
                        pe.wait_ge(*oe(i, g))
                    else:
                        pe.wait_ge(*(neg(i, 4) if first else oe(i - 1, NG)))
                    pe_turn_max(pe, *((i, g + 1) if g + 1 < NG else (i + 1, 0)))
                if h == 0:
                    pe.wait_ge(*(qr(i, 4) if first else on(i - 1, 3)))
                    pe_values(pe, i)
                if h == 1 and not last:
                    pe.wait_ge(*ve(i, 2))
                    pe_turn_ln(pe, i + 1)
                if h == 2 and not first:
                    pe.wait_ge(*(ve(i, 2) if last else hTf(i + 1, 2)))
                    pe_turn_o(pe, i - 1, 3, SIDE_B)
                if h == 3 and not last:
                    pe.wait_ge(*hTl(i + 1, DK))
                    pe_qk(pe, 0)
                    if not first:
                        pe.wait_ge(*on(i - 1, NG))
                    pe_qk(pe, 1)
                if h == 4 and not last:
                    for n in range(2):
                        pe.wait_ge(*qr(i + 1, n + 1))
                        pe_qk(pe, 2 + n)
                if h == 5 and not first:
                    for f in range(DK):
                        pe.wait_ge(*(ve(i, 2) if last else qr(i + 1, 3 + f)))
                        pe_turn_tok(pe, i - 1, f)
                if h == 6:
                    pe.wait_ge(*(qr(i + 1, 4) if first else yl(i - 1, 2)))
                    pe_turn_o(pe, i, 0, SIDE_B)
                if h == 7 and not first:
                    pe_out(pe, i - 1, 0)
                if h == 8 and not first:
                    pe.wait_ge(*on(i, 1))
                    pe_out(pe, i - 1, 1)
                if h == 9:
                    pe.wait_ge(*(qr(i + 1, 3) if first else dl(i - 1, 1)))
                    pe_turn_o(pe, i, 1, SIDE_A)
                    if not first:
                        pe_turn_delta(pe, i - 1, 0)
                if h == 10 and not first:
                    pe.wait_ge(*xs(i - 1, 1))
                    pe_turn_delta(pe, i - 1, 1)
                if h == 13:
                    pe.wait_ge(*on(i, 2))
                    pe_turn_o(pe, i, 2, SIDE_A)
                if h == 14:
                    pe.wait_ge(*(on(i, 1) if first else xs(i - 1, 2)))

        @block.tensor
        def _(pe):
            pe_turn_ln(pe, 0)
            pe.wait_ge(*hTl(0, DK))
            pe_qk(pe, 0)
            pe_qk(pe, 1)
            for n in range(2):
                pe.wait_ge(*qr(0, n + 1))
                pe_qk(pe, 2 + n)
            for h in range(AHEAD):
                for f in range(3):
                    pe_max(pe, 0, h, f)
            pe_turn_max(pe, 0, 0)
            pe.wait_ge(const.sem, 3)
            pe_batch(pe, 0, True, False)
            with pe.Fori(1, NB - 1) as i:
                pe_batch(pe, i, False, False)
            pe_batch(pe, NB - 1, False, True)
            b = NB - 1
            pe_pv(pe, b, NG - 1)
            pe.wait_ge(*xs(b - 1, 2))
            pe_turn_o(pe, b, NG - 1, SIDE_B)
            for f in range(DK):
                pe_turn_tok(pe, b, f)
            for m in range(DK):
                pe_out(pe, b, m)
            for n in range(2):
                if n:
                    pe.wait_ge(*xs(b, n))
                pe_turn_delta(pe, b, n)

        def dve_stats(dve, b):
            for n in range(TT):
                tile = x[:, bass.ds(b * TT + n, 1), :].rearrange("p a d -> p (a d)")
                dve.bn_stats(stats[:, n, :], tile).then_inc(s_stat.sem, 1)
            for n in range(TT):
                dve.wait_ge(*s_stat(b, n + 1))
                dve.nop(nofuse=True)
                dve.bn_aggr(moments[:, n, :], stats[:, n, :]).then_inc(s_mom.sem, 1)
            dve.wait_ge(*s_mom(b, TT))
            dve.tensor_scalar(var_eps[:, :], moments[:, :, 1], EPS, None, ALU.add).then_inc(s_eps.sem, 1)

        def dve_norm(dve, b, first=False):
            if not first:
                dve.wait_ge(*lnt(b - 1, 1))
            dve.wait_ge(*s_pow(b, 1))
            for n in range(TT):
                tile = x[:, bass.ds(b * TT + n, 1), :].rearrange("p a d -> p (a d)")
                dve.tensor_scalar(xn[:, n, :], tile, moments[:, n, 0:1], rstd[:, n:n + 1],
                                  ALU.subtract, ALU.mult).then_inc(s_xn.sem, 1)

        def dve_max(dve, b, h, fills=(0, 1, 2)):
            for f in fills:
                tiles, n = MAX_TILES[f], 3 * h + f
                dve.wait_ge(*mxp(b, n + 1))
                for qt, col in tiles:
                    w = (qt + 1) * P
                    dve.tensor_reduce(top[:, h, qt:qt + 1], bank(MAX0 + n % 2)[:, col:col + w], AX.X,
                                      ALU.max).then_inc(mxr.sem, 1)

        def dve_hT_lo(dve, b):
            for f in range(DK):
                dve.wait_ge(*hTh(b, f + 1))
                dve.tensor_tensor(hT_s[1][:, f, :], hT[:, f, :], hT_s[0][:, f, :].bitcast(F32),
                                  ALU.subtract).then_inc(hTl.sem, 1)

        def dve_neg_max(dve, b, g, first=False):
            src, k = bank(PV_BANK)[0:HEADS, 0:P], 4 * g
            dve.wait_ge(*mtp(b, g + 1))
            if g or not (first or (isinstance(b, int) and b == 0)):
                dve.wait_ge(*(row[g - 1](b, 48) if g else row[NG - 1](b - 1, 48)))
            dve.tensor_scalar(neg_top[:, 0, :], src, -1.0, None, ALU.mult).then_inc(neg.sem, 1)
            dve.wait_ge(*neg(b, k + 1))
            dve.scalar_tensor_tensor(neg_rest[:, :], src, -1.0, neg_top[:, 0, :], ALU.mult,
                                     ALU.subtract).then_inc(neg.sem, 1)
            dve.wait_ge(*neg(b, k + 2))
            dve.tensor_copy(neg_top[:, 1, :], neg_rest[:, :]).then_inc(neg.sem, 1)
            dve.wait_ge(*neg(b, k + 3))
            dve.tensor_tensor(neg_top[:, 2, :], neg_rest[:, :], neg_top[:, 1, :], ALU.subtract).then_inc(neg.sem, 1)

        def dve_normal(dve, b, g, side):
            src = bank(side).rearrange("p (q h c) -> p q h c", q=TT, h=GROUP)
            dve.wait_ge(*otp(b, g + 1))
            if g or not (isinstance(b, int) and b == 0):
                dve.wait_ge(*(on(b, g) if g else on(b - 1, NG)))
            dve.reciprocal(recip[:, :, :], src[:, :, :, HD]).then_inc(rc.sem, 1)
            dve.wait_ge(*rc(b, g + 1))
            out = o_tok[:, :, g * GROUP * HD:(g + 1) * GROUP * HD].rearrange("p q (h c) -> p q h c", h=GROUP)
            dve.tensor_tensor(out, src[:, :, :, 0:HD], recip[:, :, :].unsqueeze(3).to_broadcast([P, TT, GROUP, HD]),
                              ALU.mult).then_inc(on.sem, 1)

        def dve_qk_rest(dve, b, n):
            dve.wait_ge(*q1(b, n + 1))
            if n >= 2:
                dve.wait_ge(*q3(b, n - 1))
            else:
                dve.wait_ge(*hTl(b, DK))
            dve.tensor_tensor(rest[:, n % 2, :], bank((SIDE_A, SIDE_B)[n % 2]), qk_parts[n // 2][:, 0, n % 2, :],
                              ALU.subtract).then_inc(qr.sem, 1)

        def dve_o_lo(dve, b):
            for f in range(DK):
                dve.wait_ge(*yh(b, f + 1))
                dve.tensor_tensor(o_s[1][:, f, :], bank((SIDE_A, SIDE_B)[f]), o_s[0][:, f, :].bitcast(F32),
                                  ALU.subtract).then_inc(yl.sem, 1)

        def dve_add(dve, b, n):
            dve.wait_ge(*hp(b, n + 1))
            tiles = x[:, bass.ds(b * TT + 2 * n, 2), :]
            dve.tensor_tensor(tiles, tiles, bank(SIDE_B).rearrange("p (a d) -> p a d", a=2), ALU.add).then_inc(xs.sem, 1)

        def dve_batch(dve, i, first, last, norm):
            for h in range(HEADS):
                if h == 2 and not last:
                    dve_max(dve, i, h + AHEAD, (0, 1))
                    dve_hT_lo(dve, i + 1)
                    dve_max(dve, i, h + AHEAD, (2,))
                elif h + AHEAD < HEADS:
                    dve_max(dve, i, h + AHEAD)
                elif not last:
                    dve_max(dve, i + 1, h + AHEAD - HEADS)
                if h % GROUP == 1 and not (last and h + GROUP > HEADS):
                    g = h // GROUP
                    dve_neg_max(dve, *((i, g + 1) if g + 1 < NG else (i + 1, 0)))
                if h == 2 and not first:
                    dve_normal(dve, i - 1, 3, SIDE_B)
                if h in (3, 4) and not last:
                    for n in range(2):
                        dve_qk_rest(dve, i + 1, 2 * (h - 3) + n)
                if h == 5 and not first:
                    dve_o_lo(dve, i - 1)
                if h == 6:
                    dve_normal(dve, i, 0, SIDE_B)
                if h == 9:
                    dve_normal(dve, i, 1, SIDE_A)
                    if not first:
                        dve_add(dve, i - 1, 0)
                if h == 10 and not first:
                    dve_add(dve, i - 1, 1)
                if h == 8 and norm:
                    dve_stats(dve, i + 2)
                if h == 11 and norm:
                    dve_norm(dve, i + 2)
                if h == 13:
                    dve_normal(dve, i, 2, SIDE_A)

        @block.vector
        def _(dve):
            dve_stats(dve, 0)
            dve_norm(dve, 0, True)
            dve_hT_lo(dve, 0)
            dve_stats(dve, 1)
            dve_norm(dve, 1)
            for n in range(4):
                dve_qk_rest(dve, 0, n)
            dve.memset(k_stack[STACK:STACK + 3, :, :], 1.0).then_inc(const.sem, 1)
            dve.memset(values[:, :, :, HD:HD + 1], 1.0).then_inc(const.sem, 1)
            dve.memset(values[:, :, :, HD + 1:], 0.0).then_inc(const.sem, 1)
            for h in range(AHEAD):
                dve_max(dve, 0, h)
            dve_neg_max(dve, 0, 0, True)
            dve_batch(dve, 0, True, False, True)
            with dve.Fori(1, NB - 2) as i:
                dve_batch(dve, i, False, False, True)
            dve_batch(dve, NB - 2, False, False, False)
            dve_batch(dve, NB - 1, False, True, False)
            b = NB - 1
            dve_normal(dve, b, NG - 1, SIDE_B)
            dve_o_lo(dve, b)
            for n in range(2):
                dve_add(dve, b, n)
            dve.wait_ge(*xs(b, 2))

        def act_exp(act, b, h, first):
            g = h // GROUP - (1 if h % GROUP == 0 else 0)
            if g > 0:
                act.wait_ge(*pv(b, g))
            elif not first:
                act.wait_ge(*pv(b - 1, NG + g))
            for f, w in enumerate((512, 512, 256)):
                act.wait_ge(*stp(b, 3 * h + f + 1))
                act.activation(probs[:, slot(h), 512 * f:512 * f + w], bank(f)[:, 0:w], ACT.Exp).then_inc(ex.sem, 1)

        def act_keep_oT(act, b, g):
            act.wait_ge(*pv(b, g + 1))
            if not (isinstance(b, int) and b == 0 and g == 0):
                act.wait_ge(*(otp(b, g) if g else otp(b - 1, NG)))
            act.activation(oT[:, :], bank(PV_BANK), ACT.Copy).then_inc(oe.sem, 1)

        def act_values(act, b):
            for n in range(2):
                act.wait_ge(*vp(b, n + 1))
                act.activation(values[:, 2 * n:2 * n + 2, :, 0:HD].rearrange("p a h c -> p a h c"),
                               bank((SIDE_A, SIDE_B)[n]).rearrange("p (a h c) -> p a h c", a=2, h=HEADS),
                               ACT.Copy).then_inc(ve.sem, 1)

        def act_hT(act, b):
            act.wait_ge(*lnt(b, 1))
            if not (isinstance(b, int) and b == 0):
                act.wait_ge(*q3(b - 1, 4))
            act.nop(nofuse=True)
            for f in range(DK):
                act.activation(hT[:, f, :], bank((SIDE_A, SIDE_B)[f]), ACT.Identity,
                               bias=mod[:, SHIFT_A + f, bass.ds(b, 1)],
                               scale=mod[:, SCALE_A + f, bass.ds(b, 1)]).then_inc(hTf.sem, 1)
            for f in range(DK):
                act.wait_ge(*hTf(b, f + 1))
                act.activation(hT_s[0][:, f, :], hT[:, f, :], ACT.Copy).then_inc(hTh.sem, 1)

        def act_qk(act, b, n):
            act.wait_ge(*qp(b, n + 1))
            if n == 0 and not (isinstance(b, int) and b == 0):
                act.wait_ge(*stored(b - 1, 32))
            act.activation(qk_parts[n // 2][:, 0, n % 2, :], bank((SIDE_A, SIDE_B)[n % 2]), ACT.Copy).then_inc(q1.sem, 1)

        def act_qk2(act, b, n):
            act.wait_ge(*qr(b, n + 1))
            act.activation(qk_parts[n // 2][:, 1, n % 2, :], rest[:, n % 2, :], ACT.Copy).then_inc(q2.sem, 1)

        def act_o_hi(act, b):
            for f in range(DK):
                act.wait_ge(*yp(b, f + 1))
                act.activation(o_s[0][:, f, :], bank((SIDE_A, SIDE_B)[f]), ACT.Copy).then_inc(yh.sem, 1)

        def act_delta(act, b, m):
            act.wait_ge(*wp(b, m + 1))
            act.nop(nofuse=True)
            act.activation(delta[:, m, :], bank((SIDE_A, SIDE_B)[m]), ACT.Copy,
                           scale=mod[:, GATE_A + m, bass.ds(b, 1)]).then_inc(dl.sem, 1)

        def act_batch(act, i, first, last):
            for h in range(HEADS):
                act_exp(act, i, h, first)
                if h % GROUP == 0 and not (first and h == 0):
                    act_keep_oT(act, *((i, h // GROUP - 1) if h else (i - 1, NG - 1)))
                if h == 0:
                    act_values(act, i)
                if h == 1 and not last:
                    act_hT(act, i + 1)
                if h in (3, 4) and not last:
                    for n in range(2):
                        act_qk(act, i + 1, 2 * (h - 3) + n)
                    for n in range(2):
                        act_qk2(act, i + 1, 2 * (h - 3) + n)
                if h == 5 and not first:
                    act_o_hi(act, i - 1)
                if h in (7, 8) and not first:
                    act_delta(act, i - 1, h - 7)

        @block.scalar
        def _(act):
            act_hT(act, 0)
            for m in range(2):
                for n in range(2):
                    act_qk(act, 0, 2 * m + n)
                for n in range(2):
                    act_qk2(act, 0, 2 * m + n)
            act_batch(act, 0, True, False)
            with act.Fori(1, NB - 1) as i:
                act_batch(act, i, False, False)
            act_batch(act, NB - 1, False, True)
            b = NB - 1
            act_keep_oT(act, b, NG - 1)
            act_o_hi(act, b)
            for m in range(DK):
                act_delta(act, b, m)

        def pool_rstd(pool, b):
            pool.wait_ge(*s_eps(b, 1))
            pool.tensor_tensor(rstd[:, :], var_eps[:, :], mem["neg_half"][:, :], ALU.pow).then_inc(s_pow.sem, 1)

        def pool_qk3(pool, b):
            for n in range(4):
                pool.wait_ge(*q2(b, n + 1))
                pool.tensor_tensor(qk_parts[n // 2][:, 2, n % 2, :], rest[:, n % 2, :], qk_parts[n // 2][:, 1, n % 2, :],
                                   ALU.subtract).then_inc(q3.sem, 1)

        @block.gpsimd
        def _(pool):
            pool_rstd(pool, 0)
            pool_rstd(pool, 1)
            pool_qk3(pool, 0)
            with pool.Fori(0, NB - 2) as i:
                pool_qk3(pool, i + 1)
                pool_rstd(pool, i + 2)
            pool_qk3(pool, NB - 1)

        def sp_store(sp, b, side):
            if side == 0 and not (isinstance(b, int) and b == 0):
                sp.wait_ge(*loaded[NG - 1](b - 1, loaded[0].per))
            sp.wait_ge(*q3(b, 2 * side + 2))
            for j in range(3):
                for m in range(2):
                    sp.dma_start(parts_dram[side, j, :, 8 * m:8 * m + 8, :].rearrange("c h t -> h c t"),
                                 qk_parts[side][:, j, m, :]).then_inc(stored.sem, 16)

        def sp_load(sp, b, g):
            if not (isinstance(b, int) and b == 0):
                sp.wait_ge(*stp(b - 1, 3 * GROUP * (g + 1)))
            if g == 0:
                sp.wait_ge(*stored(b, stored.per))
            for side, n, parts in LOADS:
                src = parts_dram[side, parts, :, GROUP * g:GROUP * (g + 1), :]
                if src.shape[0] == 1 and n[1] - n[0] > 1:
                    src = src.to_broadcast([n[1] - n[0], HD, GROUP, T])
                sp.dma_start((q_stack, k_stack)[side][n[0] * HD:n[1] * HD, GROUP * g:GROUP * (g + 1), :], src
                             ).then_inc(loaded[g].sem, 16)

        def sp_row(sp, b, g):
            sp.wait_ge(*neg(b, 4 * (g + 1)))
            for j in range(3):
                sp.dma_start(q_stack[STACK + j:STACK + j + 1, GROUP * g:GROUP * (g + 1), :].rearrange(
                    "a h (q p) -> a (h q) p", p=P), neg_top[:, j, :]).then_inc(row[g].sem, 16)

        def sp_batch(sp, i, last):
            sp_row(sp, i, 1)
            if not last:
                sp_store(sp, i + 1, 0)
                sp_store(sp, i + 1, 1)
            sp_row(sp, i, 2)
            if not last:
                sp_load(sp, i + 1, 0)
                sp_load(sp, i + 1, 1)
            sp_row(sp, i, 3)
            if not last:
                sp_load(sp, i + 1, 2)
                sp_row(sp, i + 1, 0)
                sp_load(sp, i + 1, 3)

        @block.sync
        def _(sp):
            sp_store(sp, 0, 0)
            sp_store(sp, 0, 1)
            for g in range(NG):
                sp_load(sp, 0, g)
            sp_row(sp, 0, 0)
            with sp.Fori(0, NB - 1) as i:
                sp_batch(sp, i, False)
            sp_batch(sp, NB - 1, True)



EXPERTS = 8
CAP = NB * T // EXPERTS
SLOTS = CAP // P
CHUNKS = CAP // T
FF = 682
FK = -(-FF // P)
PER_GROUP = 2
GROUPS = EXPERTS // PER_GROUP
SEQ = NB * T // 512
ROUNDS = 15
ROW = D + EXPERTS + D


def router_stage(nc, t, ps, mem, rows_dram, logits):
    x, ident, mod = mem["x"], mem["ident"], mem["mod1"]
    with ExitStack() as ctx:
        def sb(name, shape, dt=F32):
            return ctx.enter_context(nc.sbuf_tensor("ro_" + name, shape, dt))

        def signal(name, per=1, before=0):
            return Signal(ctx, nc, "ro_" + name, per, before)

        w_r, b_r = sb("w_r", [P, DK, EXPERTS]), sb("b_r", [P, EXPERTS])
        ones = sb("ones", [P, P])
        diag = [sb(f"diag{u}", [P, DK, P]) for u in range(2)]
        gate_row = [sb(f"gate_row{u}", [P, D]) for u in range(2)]
        stats, moments, var_eps, rstd, xn = ([sb(f"{n}{u}", [P, TT] + tail) for u in range(2)] for n, tail in (
            ("stats", [6]), ("moments", [2]), ("var_eps", []), ("rstd", []), ("xn", [D])))
        hT = [sb(f"hT{u}", [P, DK, T]) for u in range(2)]
        h_tok = [sb(f"h_tok{u}", [P, TT, D]) for u in range(2)]
        small, filled = signal("small"), signal("ones")
        s_stat, s_mom, s_eps = signal("stat", TT), signal("moments", TT), signal("eps")
        s_pow, s_xn = signal("rstd"), signal("xn", TT)
        lnt, hTf, lgp, lgs, bp, be = (signal(n) for n in (
            "ln_turned", "hT", "logit_product", "logits", "turned_back", "h_kept"))
        dg, gp, gk = (signal(n) for n in ("diag", "gate_product", "gate_kept"))
        stored = [signal(f"stored{u}", 32) for u in range(2)]
        block = ctx.enter_context(nc.Block())

        @block.sync
        def _(sp):
            sp.dma_start(w_r[:, :, :], t["w_r"].rearrange("(k p) n -> p k n", p=P)).then_inc(small.sem, 16)
            sp.dma_start(b_r[:, :], t["b_r"].partition_broadcast(P)).then_inc(small.sem, 16)
            with sp.Fori(0, NB // 2) as i:
                for u in range(2):
                    b = 2 * i + u
                    sp.wait_ge(*be(b, 1))
                    sp.dma_start(rows_dram[bass.ds(b * T, T), 0:D].rearrange("(n p) d -> p n d", p=P),
                                 h_tok[u][:, :, :]).then_inc(stored[u].sem, 16)
                    sp.wait_ge(*gk(b, 1))
                    sp.dma_start(rows_dram[bass.ds(b * T, T), D + EXPERTS:ROW].rearrange("(n p) d -> p n d", p=P),
                                 gate_row[u][:, :].unsqueeze(1).to_broadcast([P, TT, D])).then_inc(stored[u].sem, 16)
            for u in range(2):
                sp.wait_ge(*stored[u](NB // 2 - 1, 32))

        @block.tensor
        def _(pe):
            def turn(b, u, first):
                pe.wait_ge(*s_xn(b, TT))
                if not first:
                    pe.wait_ge(*lgs(b - 2, 1))
                    pe.wait_ge(*gk(b - 2, 1))
                for f in range(DK):
                    for n in range(TT):
                        last = pe.transpose(ps[:, 4 * u + f, n * P:(n + 1) * P], xn[u][:, n, f * P:(f + 1) * P], ident[:, :])
                last.then_inc(lnt.sem, 1)

            def route(b, u, first):
                pe.wait_ge(*hTf(b, 1))
                for n in range(TT):
                    for k in range(DK):
                        last = pe.matmul(ps[:, 4 * u, n * EXPERTS:(n + 1) * EXPERTS], hT[u][:, k, n * P:(n + 1) * P],
                                         w_r[:, k, :], start=(k == 0), stop=(k == DK - 1))
                last.then_inc(lgp.sem, 1)
                pe.wait_ge(*dg(b, 1))
                for f in range(DK):
                    last = pe.matmul(ps[:, 4 * u + 1, f * P:(f + 1) * P], ones[:, :], diag[u][:, f, :],
                                     start=True, stop=True)
                last.then_inc(gp.sem, 1)
                if not first:
                    pe.wait_ge(*be(b - 2, 1))
                for n in range(TT):
                    for f in range(DK):
                        last = pe.transpose(ps[:, 4 * u + 2 + n // 2, (n % 2) * D + f * P:(n % 2) * D + (f + 1) * P],
                                            hT[u][:, f, n * P:(n + 1) * P], ident[:, :])
                last.then_inc(bp.sem, 1)

            pe.wait_ge(small.sem, 32)
            pe.wait_ge(filled.sem, 1)
            turn(0, 0, True)
            turn(1, 1, True)
            route(0, 0, True)
            turn(2, 0, False)
            route(1, 1, True)
            with pe.Fori(1, NB // 2 - 1) as i:
                turn(2 * i + 1, 1, False)
                route(2 * i, 0, False)
                turn(2 * i + 2, 0, False)
                route(2 * i + 1, 1, False)
            turn(NB - 1, 1, False)
            route(NB - 2, 0, False)
            route(NB - 1, 1, False)

        @block.vector
        def _(dve):
            def statistics(b, u):
                for n in range(TT):
                    tile = x[:, bass.ds(b * TT + n, 1), :].rearrange("p a d -> p (a d)")
                    dve.bn_stats(stats[u][:, n, :], tile).then_inc(s_stat.sem, 1)
                for n in range(TT):
                    dve.wait_ge(*s_stat(b, n + 1))
                    dve.nop(nofuse=True)
                    dve.bn_aggr(moments[u][:, n, :], stats[u][:, n, :]).then_inc(s_mom.sem, 1)
                dve.wait_ge(*s_mom(b, TT))
                dve.tensor_scalar(var_eps[u][:, :], moments[u][:, :, 1], EPS, None, ALU.add).then_inc(s_eps.sem, 1)

            def norm(b, u, first):
                if not first:
                    dve.wait_ge(*lnt(b - 2, 1))
                dve.wait_ge(*s_pow(b, 1))
                for n in range(TT):
                    tile = x[:, bass.ds(b * TT + n, 1), :].rearrange("p a d -> p (a d)")
                    dve.tensor_scalar(xn[u][:, n, :], tile, moments[u][:, n, 0:1], rstd[u][:, n:n + 1],
                                      ALU.subtract, ALU.mult).then_inc(s_xn.sem, 1)

            def keep_logits(b, u):
                dve.wait_ge(*lgp(b, 1))
                dve.tensor_tensor(logits[:, bass.ds(b * TT, TT), :],
                                  ps[:, 4 * u, 0:TT * EXPERTS].rearrange("p (n e) -> p n e", e=EXPERTS),
                                  b_r[:, :].unsqueeze(1).to_broadcast([P, TT, EXPERTS]), ALU.add).then_inc(lgs.sem, 1)

            dve.wait_ge(small.sem, 32)
            statistics(0, 0)
            statistics(1, 1)
            norm(0, 0, True)
            dve.wait_ge(*s_xn(0, TT))
            statistics(2, 0)
            norm(1, 1, True)
            with dve.Fori(0, NB // 2 - 2) as i:
                for u in range(2):
                    b = 2 * i + u
                    dve.wait_ge(*s_xn(b + 1, TT))
                    statistics(b + 3, 1 - u)
                    norm(b + 2, u, False)
                    keep_logits(b, u)
            b = NB - 4
            dve.wait_ge(*s_xn(b + 1, TT))
            statistics(b + 3, 1)
            for u in range(2):
                norm(b + 2 + u, u, False)
                keep_logits(b + u, u)
            for u in range(2):
                keep_logits(b + 2 + u, u)
            dve.wait_ge(*lgs(NB - 1, 1))

        @block.gpsimd
        def _(pool):
            def steps(b, u, first):
                pool.wait_ge(*s_eps(b, 1))
                pool.tensor_tensor(rstd[u][:, :], var_eps[u][:, :], mem["neg_half"][:, :], ALU.pow
                                   ).then_inc(s_pow.sem, 1)
                if not first:
                    pool.wait_ge(*gp(b - 2, 1))
                pool.nop(nofuse=True)
                for f in range(DK):
                    last = pool.tensor_tensor(diag[u][:, f, :], ident[:, :],
                                              mod[:, GATE_B + f, bass.ds(b, 1)].to_broadcast([P, P]), ALU.mult)
                last.then_inc(dg.sem, 1)

            pool.memset(ones[:, :], 1.0).then_inc(filled.sem, 1)
            for u in range(2):
                steps(u, u, True)
            with pool.Fori(1, NB // 2) as i:
                for u in range(2):
                    steps(2 * i + u, u, False)

        @block.scalar
        def _(act):
            def modulate(b, u, first):
                act.wait_ge(*lnt(b, 1))
                if not first:
                    act.wait_ge(*bp(b - 2, 1))
                act.nop(nofuse=True)
                for f in range(DK):
                    last = act.activation(hT[u][:, f, :], ps[:, 4 * u + f, :], ACT.Identity,
                                          bias=mod[:, SHIFT_B + f, bass.ds(b, 1)],
                                          scale=mod[:, SCALE_B + f, bass.ds(b, 1)])
                last.then_inc(hTf.sem, 1)

            def keep_h(i, u, first):
                act.wait_ge(*gp(2 * i + u, 1))
                if not first:
                    act.wait_ge(*stored[u](i - 1, 32))
                act.activation(gate_row[u][:, :], ps[:, 4 * u + 1, 0:D], ACT.Copy).then_inc(gk.sem, 1)
                act.wait_ge(*bp(2 * i + u, 1))
                act.activation(h_tok[u][:, :, :].rearrange("p n d -> p (n d)"),
                               ps[:, 4 * u + 2:4 * u + 4, :].rearrange("p k n -> p (k n)"), ACT.Copy).then_inc(be.sem, 1)

            modulate(0, 0, True)
            modulate(1, 1, True)
            keep_h(0, 0, True)
            modulate(2, 0, False)
            keep_h(0, 1, True)
            with act.Fori(1, NB // 2 - 1) as i:
                modulate(2 * i + 1, 1, False)
                keep_h(i, 0, False)
                modulate(2 * i + 2, 0, False)
                keep_h(i, 1, False)
            modulate(NB - 1, 1, False)
            keep_h(NB // 2 - 1, 0, False)
            keep_h(NB // 2 - 1, 1, False)


def choose_stage(nc, t, ps, mem, rows_dram, logits, index, staging, out):
    ident = mem["ident"]
    with ExitStack() as ctx:
        def sb(name, shape, dt=F32):
            return ctx.enter_context(nc.sbuf_tensor("ch_" + name, shape, dt))

        def sem(name):
            return ctx.enter_context(nc.semaphore("ch_" + name))

        top, total = sb("top", [P, NT]), sb("total", [P, NT])
        prob = sb("prob", [P, NT, EXPERTS])
        by_expert = sb("by_expert", [P, TT, EXPERTS, SEQ])
        val = sb("val", [P, T])
        trials, units = sb("trials", [P, ROUNDS, 3], I32), sb("units", [P, ROUNDS])
        thr, cand, step = sb("thr", [P, 1], I32), sb("cand", [P, 3], I32), sb("step", [P, 1], I32)
        reached, n_reached = sb("reached", [P, 3]), sb("n_reached", [P, 1])
        same, before = sb("same", [P, P]), sb("before", [P, P])
        hit = [sb(f"hit{c}", [P, T]) for c in range(3)]
        count = sb("count", [P, 3])
        above, equal, upto = sb("above", [P, T]), sb("equal", [P, T]), sb("upto", [P, T])
        ones = sb("ones", [P, T])
        counts = sb("counts", [P, 2])
        limit, offset = sb("limit", [P, 1]), sb("offset", [P, 1])
        chosen, place = sb("chosen", [P, T]), sb("place", [P, T])
        pos = sb("pos", [P, TT, EXPERTS, SEQ])
        high_i, high = sb("high_i", [P, TT * P], I32), sb("high", [P, TT, EXPERTS, SEQ])
        low = sb("low", [P, TT, EXPERTS, SEQ])
        iota_f = sb("iota", [P, P])
        iota_b = sb("iota_b", [P, P], BF16)
        low_b = sb("low_b", [P, TT, EXPERTS, SEQ], BF16)
        p_col = sb("p_col", [P, 1])
        tile_no = sb("tile_no", [P, TT, SEQ])
        one_hot = sb("one_hot", [P, SEQ * EXPERTS * SLOTS])
        facts = sb("facts", [P, TT, SEQ, EXPERTS, 2, SLOTS], BF16)
        match = [sb(f"match{j}", [P, EXPERTS, P], BF16) for j in range(TT)]
        number = sb("number", [P, EXPERTS, SLOTS])

        consts, s, e1, turned, cnt, counted, made, took, done = (sem(n) for n in (
            "consts", "steps", "exp", "turned", "count", "counted", "made", "took", "done"))
        m_sems = [sem(f"match{j}") for j in range(TT)]
        u_sems = [sem(f"used{j}") for j in range(TT)]
        stored, sums = sem("stored"), sem("sums_started")
        tested = sem("tested")
        block = ctx.enter_context(nc.Block())
        n_consts = 7
        steps = {}

        @block.sync
        def _(sp):
            sp.dma_start(trials[:, :, :], t["trials"]).then_inc(consts, 16)
            for dst, name in ((units, "units"), (same, "same_expert"), (before, "before"),
                              (iota_f, "iota"), (p_col, "p_col")):
                sp.dma_start(dst[:, :], t[name]).then_inc(consts, 16)
            sp.dma_start(tile_no[:, :, :], t["tile_no"]).then_inc(consts, 16)
            sp.dma_start(out.rearrange("b (n p) d -> p (b n) d", p=P), mem["x"][:, :, :]).then_inc(sums, 16)
            sp.wait_ge(s, 6)
            with nc.allow_non_contiguous_dma(reason="eight probabilities a row"):
                for n in range(4):
                    sp.dma_start(rows_dram[n * 2048:(n + 1) * 2048, D:D + EXPERTS].rearrange("(n p) e -> p n e", p=P),
                                 prob[:, n * 16:(n + 1) * 16, :]).then_inc(stored, 16)
            load_up(sp, t, staging, 0)
            for e in range(PER_GROUP):
                load_down(sp, t, staging, 0, e)
            sp.wait_ge(stored, 64)
            sp.wait_ge(sums, 16)

        @block.scalar
        def _(act):
            act.wait_ge(s, 2)
            act.activation(prob[:, :, :], prob[:, :, :], ACT.Exp).then_inc(e1, 1)

        @block.vector
        def _(dve):
            n = [0]

            def then(ins):
                n[0] += 1
                ins.then_inc(s, 1)
                dve.wait_ge(s, n[0])

            then(dve.tensor_reduce(top[:, :], logits[:, :, :], AX.X, ALU.max))
            then(dve.tensor_tensor(prob[:, :, :], logits[:, :, :], top[:, :].unsqueeze(2).to_broadcast([P, NT, EXPERTS]),
                                   ALU.subtract))
            dve.wait_ge(e1, 1)
            then(dve.tensor_reduce(total[:, :], prob[:, :, :], AX.X, ALU.add))
            then(dve.reciprocal(total[:, :], total[:, :]))
            then(dve.tensor_tensor(prob[:, :, :], prob[:, :, :], total[:, :].unsqueeze(2).to_broadcast([P, NT, EXPERTS]),
                                   ALU.mult))
            for j in range(TT):
                ins = dve.tensor_copy(by_expert[:, j, :, :],
                                      prob[:, :, :].rearrange("p (c j) e -> p j e c", j=TT)[:, j, :, :])
                ins.then_inc(s, 1)
            n[0] += TT
            dve.wait_ge(s, n[0])
            dve.wait_ge(turned, 1)
            then(dve.tensor_copy(val[:, :], ps[:, 0, :]))
            dve.wait_ge(consts, 16 * n_consts)
            then(dve.memset(thr[:, :], 0))
            then(dve.memset(ones[:, :], 1.0))
            then(dve.tensor_copy(iota_b[:, :], iota_f[:, :]))
            base = n[0]
            with dve.Fori(0, ROUNDS) as i:
                dve.wait_ge(s, i * 3 + base)
                dve.nop(nofuse=True)
                dve.tensor_tensor(cand[:, :], thr[:, 0:1].to_broadcast([P, 3]),
                                  trials[:, bass.ds(i, 1), :].rearrange("p a c -> p (a c)"), ALU.bitwise_or
                                  ).then_inc(tested, 1)
                dve.wait_ge(tested, i + 1)
                for c in range(3):
                    dve.tensor_scalar(hit[c][:, :], val[:, :], cand[:, c:c + 1].bitcast(F32), 0.0, ALU.is_ge, ALU.add,
                                      accum_out=count[:, c:c + 1]).then_inc(cnt, 1)
                dve.wait_ge(counted, i + 1)
                dve.tensor_scalar(reached[:, :], ps[:, 1, 0:3], float(CAP), 0.0, ALU.is_ge, ALU.add,
                                  accum_out=n_reached[:, :]).then_inc(s, 1)
                dve.wait_ge(s, i * 3 + (base + 1))
                dve.tensor_scalar(step[:, :], n_reached[:, :], units[:, bass.ds(i, 1)], None, ALU.mult).then_inc(s, 1)
                dve.wait_ge(s, i * 3 + (base + 2))
                dve.tensor_tensor(thr[:, :], thr[:, :], step[:, :], ALU.bitwise_or).then_inc(s, 1)
            n[0] += 3 * ROUNDS
            dve.wait_ge(s, n[0])
            then(dve.tensor_scalar(above[:, :], val[:, :], thr[:, :].bitcast(F32), 0.0, ALU.is_gt, ALU.add,
                                   accum_out=counts[:, 0:1]))
            then(dve.tensor_scalar(equal[:, :], val[:, :], thr[:, :].bitcast(F32), 0.0, ALU.is_equal, ALU.add,
                                   accum_out=counts[:, 1:2]))
            steps["counts"] = n[0]
            then(dve.tensor_tensor_scan(upto[:, :], ones[:, :], equal[:, :], 0.0, ALU.mult, ALU.add))
            dve.wait_ge(turned, 2)
            then(dve.tensor_scalar(limit[:, :], ps[:, 2, 0:1], -1.0, float(CAP), ALU.mult, ALU.add))
            then(dve.tensor_tensor(limit[:, :], limit[:, :], ps[:, 3, 0:1], ALU.subtract))
            then(dve.scalar_tensor_tensor(chosen[:, :], upto[:, :], limit[:, 0:1], equal[:, :], ALU.is_le, ALU.mult))
            then(dve.tensor_tensor(chosen[:, :], chosen[:, :], above[:, :], ALU.add))
            then(dve.tensor_tensor_scan(upto[:, :], ones[:, :], chosen[:, :], 0.0, ALU.mult, ALU.add))
            steps["upto"] = n[0]
            dve.wait_ge(turned, 3)
            then(dve.tensor_copy(offset[:, :], ps[:, 4, 0:1]))
            then(dve.scalar_tensor_tensor(place[:, :], upto[:, :], offset[:, 0:1], chosen[:, :], ALU.add, ALU.mult))
            then(dve.tensor_scalar(place[:, :], place[:, :], -1.0, None, ALU.add))
            steps["place"] = n[0]
            dve.wait_ge(turned, 4)
            then(dve.tensor_copy(pos[:, :, :, :].rearrange("p j e c -> p (j e c)"), ps[:, 5, :]))
            flat = pos[:, :, :, :].rearrange("p j e c -> p (j e c)")
            then(dve.tensor_scalar(high_i[:, :], flat, 1.0 / P, 0.5 / P - 0.5, ALU.mult, ALU.add))
            then(dve.tensor_copy(high[:, :, :, :].rearrange("p j e c -> p (j e c)"), high_i[:, :]))
            then(dve.scalar_tensor_tensor(low_b[:, :, :, :].rearrange("p j e c -> p (j e c)"),
                                          high[:, :, :, :].rearrange("p j e c -> p (j e c)"), -float(P), flat,
                                          ALU.mult, ALU.add))
            steps["low"] = n[0]
            for j in range(TT):
                grid = one_hot[:, :].rearrange("p (c e a) -> p c e a", c=SEQ, e=EXPERTS)
                then(dve.tensor_tensor(grid, high[:, j, :, :].rearrange("p e c -> p c e").unsqueeze(3).to_broadcast(
                    [P, SEQ, EXPERTS, SLOTS]), iota_f[:, 0:SLOTS].unsqueeze(1).unsqueeze(1).to_broadcast(
                    [P, SEQ, EXPERTS, SLOTS]), ALU.is_equal))
                then(dve.tensor_tensor(facts[:, j, :, :, 0, :], grid, tile_no[:, j, :].unsqueeze(2).unsqueeze(3).to_broadcast(
                    [P, SEQ, EXPERTS, SLOTS]), ALU.mult))
                then(dve.tensor_scalar(facts[:, j, :, :, 1, :], grid, p_col[:, 0:1], None, ALU.mult))
            steps["facts"] = n[0]

            def one_hots(c, first):
                for j in range(TT):
                    if not first:
                        dve.wait_ge(u_sems[j], c)
                    dve.tensor_tensor(match[j][:, :, :], low_b[:, j, :, bass.ds(c, 1)].to_broadcast([P, EXPERTS, P]),
                                      iota_b[:, :].unsqueeze(1).to_broadcast([P, EXPERTS, P]),
                                      ALU.is_equal).then_inc(m_sems[j], 1)
            one_hots(0, True)
            with dve.Fori(1, SEQ) as c:
                one_hots(c, False)
            dve.wait_ge(done, 1)
            got = ps[:, 6, 0:EXPERTS * 2 * SLOTS].rearrange("p (e v a) -> p e v a", e=EXPERTS, v=2)
            then(dve.tensor_copy(number[:, :, :], got[:, :, 1, :]))
            then(dve.scalar_tensor_tensor(index[:, :, :], got[:, :, 0, :], float(P), number[:, :, :], ALU.mult, ALU.add))

        @block.tensor
        def _(pe):
            pe.wait_ge(s, 5 + TT)
            for j in range(TT):
                last = pe.transpose(ps[:, 0, j * P:(j + 1) * P], by_expert[:, j, :, :].rearrange("p e c -> p (e c)"),
                                    ident[:, :])
            last.then_inc(turned, 1)
            pe.wait_ge(consts, 16 * n_consts)
            with pe.Fori(0, ROUNDS) as i:
                pe.wait_ge(cnt, 3 * i + 3)
                pe.matmul(ps[:, 1, 0:3], same[:, :], count[:, :], start=True, stop=True).then_inc(counted, 1)
            pe.wait_ge(s, steps["counts"])
            pe.matmul(ps[:, 2, 0:1], same[:, :], counts[:, 0:1], start=True, stop=True)
            pe.matmul(ps[:, 3, 0:1], before[:, :], counts[:, 1:2], start=True, stop=True).then_inc(turned, 1)
            pe.wait_ge(s, steps["upto"])
            pe.matmul(ps[:, 4, 0:1], before[:, :], upto[:, T - 1:T], start=True, stop=True).then_inc(turned, 1)
            pe.wait_ge(s, steps["place"])
            for j in range(TT):
                last = pe.transpose(ps[:, 5, j * P:(j + 1) * P], place[:, j * P:(j + 1) * P], ident[:, :])
            last.then_inc(turned, 1)
            pe.wait_ge(s, steps["facts"])

            def add_up(c, first, final):
                for j in range(TT):
                    pe.wait_ge(m_sems[j], c + 1)
                    for e in range(EXPERTS):
                        w = 2 * SLOTS
                        rhs = facts[:, j, bass.ds(c, 1), e, :, :].rearrange("p c v a -> p (c v a)")
                        last = pe.matmul(ps[:, 6, e * w:(e + 1) * w], match[j][:, e, :], rhs,
                                         start=(first and j == 0 and e == 0), stop=(final and j == TT - 1),
                                         skip_group_check=True)
                    last.then_inc(u_sems[j], 1)
                if final:
                    pe.wait_ge(u_sems[TT - 1], SEQ)
            add_up(0, True, False)
            with pe.Fori(1, SEQ - 1) as c:
                add_up(c, False, False)
            add_up(SEQ - 1, False, True)
            pe.drain().then_inc(done, 1)


def load_up(sp, t, staging, g):
    sp.dma_start(staging["f_up"][:, :, :], t["w_up"][bass.ds(g, 1), :, :].rearrange("g (k p) n -> p (g k) n", p=P)
                 ).then_inc(staging["up_in"].sem, 16)


def load_down(sp, t, staging, g, e):
    sp.dma_start(staging["f_down"][e][:, :, :], t["w_down"][bass.ds(g * PER_GROUP + e, 1), :, :].rearrange(
        "g (k p) n -> p (g k) n", p=P)).then_inc(staging["dn_in"][e].sem, 16)


def expert_stage(nc, t, ps, mem, rows_dram, index, staging, out):
    rows_out = out.rearrange("b t d -> (b t) d")
    ident = mem["ident"]
    PER_LOOP = PER_GROUP * CHUNKS
    with ExitStack() as ctx:
        def sb(name, shape, dt=F32):
            return ctx.enter_context(nc.sbuf_tensor("ex_" + name, shape, dt))

        def pair(name, shape):
            return sb(name + "_hi", shape, F32R), sb(name + "_lo", shape, F32R)

        def signal(name, per=1, before=0):
            return Signal(ctx, nc, "ex_" + name, per, before)

        f_up, f_down, up_in, dn_in = (staging[n] for n in ("f_up", "f_down", "up_in", "dn_in"))
        w_up = pair("w_up", [P, DK, FK * P])
        w_down = [pair(f"w_down{e}", [P, FK, D]) for e in range(PER_GROUP)]
        b_up = sb("b_up", [P, GROUPS, FK])
        b_down = sb("b_down", [P, EXPERTS, D])
        flat = mem["x"][:, :, :].rearrange("p n d -> p (n d)")
        tok = [flat[:, u * TT * ROW:(u + 1) * TT * ROW].rearrange("p (a r) -> p a r", a=TT) for u in range(PER_LOOP)]
        tok_s = pair("tok", [P, DK, T])
        mid = [sb(f"mid{n}", [P, T]) for n in range(3)]
        mid_s = pair("mid", [P, FK, T])
        summed = sb("summed", [P, TT, D])
        result = [sb(f"result{u}", [P, TT, D]) for u in range(2)]

        small = signal("small")
        uh, ul, dh, dlo = signal("up_hi"), signal("up_lo"), signal("down_hi", PER_GROUP), signal("down_lo", PER_GROUP)
        gath = [signal(f"gathered{u}", 16 * TT) for u in range(PER_LOOP)]
        tp, th, tl = signal("turned", DK), signal("tok_hi", DK), signal("tok_lo", DK)
        up, si, ml = (signal(n, FK) for n in ("up_product", "silu", "mid_lo"))
        mh, mh_dve = signal("mid_hi", FK // 2), signal("mid_hi_odd", FK // 2)
        dp, sm, rs = signal("down_product", 2), signal("summed", TT), signal("result", TT)
        scat = signal("scattered", 16 * TT)
        block = ctx.enter_context(nc.Block())

        def up_bank(f):
            return ps[:, 2 + f % 3, :]

        @block.gpsimd
        def _(pool):
            def gather(n, e, c):
                u = n % PER_LOOP
                if n >= PER_LOOP:
                    pool.wait_ge(*rs(n - PER_LOOP, TT))
                    pool.nop(nofuse=True)
                for a in range(TT):
                    pool.indirect_dma_start(
                        out=tok[u][:, a, :], out_offset=None, in_=rows_dram[:, :],
                        in_offset=bass.IndirectOffsetOnAxis(ap=index[:, e, c * TT + a:c * TT + a + 1], axis=0)
                    ).then_inc(gath[u].sem, 16)

            def scatter(n, e, c):
                pool.wait_ge(*rs(n, TT))
                if n:
                    pool.wait_ge(*scat(n - 1, 16 * TT))
                pool.nop(nofuse=True)
                for a in range(TT):
                    pool.indirect_dma_start(
                        out=rows_out, out_offset=bass.IndirectOffsetOnAxis(
                            ap=index[:, e, c * TT + a:c * TT + a + 1], axis=0),
                        in_=result[n % 2][:, a, :], in_offset=None, compute_op=ALU.add).then_inc(scat.sem, 16)

            order = [(n, n // CHUNKS, n % CHUNKS) for n in range(EXPERTS * CHUNKS)]
            for n in range(PER_LOOP - 1):
                gather(*order[n])
            for n, e, c in order:
                if n + PER_LOOP - 1 < len(order):
                    gather(*order[n + PER_LOOP - 1])
                scatter(n, e, c)
            pool.wait_ge(*scat(len(order) - 1, 16 * TT))

        @block.sync
        def _(sp):
            sp.dma_start(b_up[:, :, :], t["b_up"]).then_inc(small.sem, 16)
            sp.dma_start(b_down[:, :, :], t["b_down"].partition_broadcast(P)).then_inc(small.sem, 16)

            with sp.Fori(1, GROUPS) as g:
                sp.wait_ge(*ul(g - 1, 1))
                load_up(sp, t, staging, g)
                for e in range(PER_GROUP):
                    sp.wait_ge(*dlo(g - 1, e + 1))
                    load_down(sp, t, staging, g, e)

        @block.tensor
        def _(pe):
            def turn(n, u, g, first):
                pe.wait_ge(*gath[u](g, 16 * TT))
                if not first:
                    pe.wait_ge(*tl(n - 1, DK))
                for f in range(DK):
                    for a in range(TT):
                        last = pe.transpose(ps[:, f, a * P:(a + 1) * P], tok[u][:, a, f * P:(f + 1) * P], ident[:, :])
                    last.then_inc(tp.sem, 1)

            def inner(n, g, first):
                pe.wait_ge(*tl(n, DK))
                pe.wait_ge(*ul(g, 1))
                for f in range(FK):
                    if f >= 3:
                        pe.wait_ge(*si(n, f - 2))
                    elif not first:
                        pe.wait_ge(*si(n - 1, FK - 2 + f))
                    for k in range(DK):
                        last = product3(pe, up_bank(f), [w[:, k, f * P:(f + 1) * P] for w in w_up],
                                        [h[:, k, :] for h in tok_s], k == 0, k == DK - 1)
                    last.then_inc(up.sem, 1)

            def outer(n, g, e, first):
                pe.wait_ge(*dlo(g, e + 1))
                for a in range(TT):
                    if a % 2 == 0 and not first:
                        pe.wait_ge(*sm(n - 1, a + 2))
                    for k in range(FK):
                        if a == 0:
                            pe.wait_ge(*ml(n, k + 1))
                        last = product3(pe, ps[:, 6 + a // 2, (a % 2) * D:(a % 2 + 1) * D],
                                        [m[:, k, a * P:(a + 1) * P] for m in mid_s],
                                        [w[:, k, :] for w in w_down[e]], k == 0, k == FK - 1)
                    if a % 2:
                        last.then_inc(dp.sem, 1)

            def group(g, first, final):
                for m in range(PER_LOOP):
                    n = g * PER_LOOP + m
                    inner(n, g, first and m == 0)
                    if not (final and m == PER_LOOP - 1):
                        turn(n + 1, (m + 1) % PER_LOOP, g + (m + 1) // PER_LOOP, False)
                    outer(n, g, m // CHUNKS, first and m == 0)

            turn(0, 0, 0, True)
            group(0, True, False)
            with pe.Fori(1, GROUPS - 1) as g:
                group(g, False, False)
            group(GROUPS - 1, False, True)

        @block.vector
        def _(dve):
            def split_up(g):
                dve.wait_ge(*uh(g, 1))
                dve.tensor_tensor(w_up[1][:, :, :], f_up[:, :, :], w_up[0][:, :, :].bitcast(F32),
                                  ALU.subtract).then_inc(ul.sem, 1)

            def split_down(g, e):
                dve.wait_ge(*dh(g, e + 1))
                dve.tensor_tensor(w_down[e][1][:, :, :], f_down[e][:, :, :], w_down[e][0][:, :, :].bitcast(F32),
                                  ALU.subtract).then_inc(dlo.sem, 1)

            def tok_lo(n):
                for f in range(DK):
                    dve.wait_ge(*th(n, f + 1))
                    dve.tensor_tensor(tok_s[1][:, f, :], ps[:, f, :], tok_s[0][:, f, :].bitcast(F32),
                                      ALU.subtract).then_inc(tl.sem, 1)

            def group(g, first, final):
                for m in range(PER_LOOP):
                    n = g * PER_LOOP + m
                    for f in range(FK):
                        if f % 2:
                            dve.wait_ge(*si(n, f + 1))
                            dve.tensor_copy(mid_s[0][:, f, :], mid[f % 3][:, :]).then_inc(mh_dve.sem, 1)
                            dve.wait_ge(*mh_dve(n, f // 2 + 1))
                        else:
                            dve.wait_ge(*mh(n, f // 2 + 1))
                        dve.tensor_tensor(mid_s[1][:, f, :], mid[f % 3][:, :], mid_s[0][:, f, :].bitcast(F32),
                                          ALU.subtract).then_inc(ml.sem, 1)
                    if not (final and m == PER_LOOP - 1):
                        tok_lo(n + 1)
                    if not final and m == PER_LOOP - 1:
                        split_up(g + 1)
                    for a in range(TT):
                        if a % 2 == 0:
                            dve.wait_ge(*dp(n, a // 2 + 1))
                        if a == 0 and not (first and m == 0):
                            dve.wait_ge(*rs(n - 1, TT))
                        dve.tensor_tensor(summed[:, a, :], ps[:, 6 + a // 2, (a % 2) * D:(a % 2 + 1) * D],
                                          b_down[:, bass.ds(g * PER_GROUP + m // CHUNKS, 1), :].rearrange(
                                              "p e d -> p (e d)"), ALU.add).then_inc(sm.sem, 1)
                    dve.wait_ge(*gath[m](g, 16 * TT))
                    if not (first and m < 2):
                        dve.wait_ge(*scat(n - 2, 16 * TT))
                    for a in range(TT):
                        dve.wait_ge(*sm(n, a + 1))
                        dve.nop(nofuse=True)
                        dve.scalar_tensor_tensor(result[m % 2][:, a, :], summed[:, a, :],
                                                 tok[m][:, a, bass.ds(g * PER_GROUP + (D + m // CHUNKS), 1)],
                                                 tok[m][:, a, D + EXPERTS:ROW], ALU.mult, ALU.mult
                                                 ).then_inc(rs.sem, 1)
                    if not final and m == PER_LOOP - 1:
                        split_down(g + 1, 1)
                    if not final and m == CHUNKS - 1:
                        split_down(g + 1, 0)

            dve.wait_ge(small.sem, 32)
            split_up(0)
            split_down(0, 0)
            split_down(0, 1)
            tok_lo(0)
            group(0, True, False)
            with dve.Fori(1, GROUPS - 1) as g:
                group(g, False, False)
            group(GROUPS - 1, False, True)

        @block.scalar
        def _(act):
            def split_up(g):
                act.wait_ge(*up_in(g, 16))
                act.activation(w_up[0][:, :, :], f_up[:, :, :], ACT.Copy).then_inc(uh.sem, 1)

            def split_down(g, e):
                act.wait_ge(*dn_in[e](g, 16))
                act.activation(w_down[e][0][:, :, :], f_down[e][:, :, :], ACT.Copy).then_inc(dh.sem, 1)

            def tok_hi(n):
                for f in range(DK):
                    act.wait_ge(*tp(n, f + 1))
                    act.activation(tok_s[0][:, f, :], ps[:, f, :], ACT.Copy).then_inc(th.sem, 1)

            def group(g, first, final):
                for m in range(PER_LOOP):
                    n, e = g * PER_LOOP + m, m // CHUNKS
                    for f in range(FK):
                        act.wait_ge(*up(n, f + 1))
                        if f >= 3:
                            act.wait_ge(*ml(n, f - 2))
                        elif not (first and m == 0):
                            act.wait_ge(*ml(n - 1, FK - 2 + f))
                        act.nop(nofuse=True)
                        act.activation(mid[f % 3][:, :], up_bank(f), ACT.Silu,
                                       bias=b_up[:, bass.ds(g, 1), f:f + 1].rearrange("p g f -> p (g f)")
                                       ).then_inc(si.sem, 1)
                        if f == 0 and not (first and m == 0):
                            act.wait_ge(*dp(n - 1, 2))
                        if f % 2 == 0:
                            act.wait_ge(*si(n, f + 1))
                            act.activation(mid_s[0][:, f, :], mid[f % 3][:, :], ACT.Copy).then_inc(mh.sem, 1)
                    if not (final and m == PER_LOOP - 1):
                        tok_hi(n + 1)
                    if not final and m == PER_LOOP - 1:
                        split_up(g + 1)
                    if not final and m % CHUNKS == CHUNKS - 1:
                        act.wait_ge(*dp(n, 2))
                    if not final and m == PER_LOOP - 1:
                        split_down(g + 1, 1)
                    if not final and m == CHUNKS - 1:
                        split_down(g + 1, 0)

            split_up(0)
            split_down(0, 0)
            split_down(0, 1)
            tok_hi(0)
            group(0, True, False)
            with act.Fori(1, GROUPS - 1) as g:
                group(g, False, False)
            group(GROUPS - 1, False, True)


def moe_stage(nc, t, ps, mem, out):
    rows_dram = nc.dram_tensor("token_rows", (NB * T, ROW), F32, kind="Internal").ap()
    with ExitStack() as ctx:
        index = ctx.enter_context(nc.sbuf_tensor("slot_tokens", [P, EXPERTS, SLOTS], I32))
        staging = {
            "f_up": ctx.enter_context(nc.sbuf_tensor("w_up_loaded", [P, DK, FK * P], F32)),
            "f_down": [ctx.enter_context(nc.sbuf_tensor(f"w_down_loaded{e}", [P, FK, D], F32)) for e in range(PER_GROUP)],
            "up_in": Signal(ctx, nc, "ex_up_loaded", 16),
            "dn_in": [Signal(ctx, nc, f"ex_down_loaded{e}", 16) for e in range(PER_GROUP)],
        }
        with ExitStack() as ctx_l:
            logits = ctx_l.enter_context(nc.sbuf_tensor("logits", [P, NT, EXPERTS], F32))
            router_stage(nc, t, ps, mem, rows_dram, logits)
            choose_stage(nc, t, ps, mem, rows_dram, logits, index, staging, out)
        expert_stage(nc, t, ps, mem, rows_dram, index, staging, out)


def _layout(i):
    c = np.ascontiguousarray

    def col(name):
        return np.asarray(i[name]).reshape(-1, P).T

    conv_w = np.asarray(i["L0_attn_conv_w"])
    g = conv_w.shape[1]
    blocks = np.zeros((IK * TAPS, P, P), np.float32)
    for m in range(IK):
        for half in range(P // g):
            rows = slice(half * g, (half + 1) * g)
            w = conv_w[m * P + half * g:m * P + (half + 1) * g]
            for k in range(TAPS):
                blocks[m * TAPS + k, rows, rows] = w[:, :, k].T
    quads = np.zeros((P, P), np.float32)
    quads[::32, :] = 1.0
    dirs = np.zeros((HEADS, D), np.float32)
    for h in range(HEADS):
        dirs[h, h * HD:h * HD + 8] = np.asarray(i["L1_attn_head_dirs"])[h]
    later = np.triu(np.ones((P, P), bool), 1)
    masks = np.where(np.stack([later, later.T]), np.float32(-3.0e38), np.float32(0.0))
    pad = FK * P - FF
    w_up = np.pad(np.asarray(i["L1_ffn_W_up"]), ((0, 0), (0, 0), (0, pad)))
    w_down = np.pad(np.asarray(i["L1_ffn_W_down"]), ((0, 0), (0, pad), (0, 0)))
    b_up = np.pad(np.asarray(i["L1_ffn_b_up"]), ((0, 0), (0, pad))).reshape(GROUPS, FK, P).transpose(2, 0, 1)
    units = (1 << np.arange(2 * ROUNDS - 2, -1, -2)).astype(np.int32)
    row, col_no = np.arange(P)[:, None], np.arange(P)[None, :]
    same = row // SEQ == col_no // SEQ
    before = same & (row < col_no)
    a = {
        "x": i["L0_attn_hidden_states"], "ident": np.eye(P, dtype=np.float32), "quads": quads,
        "in_wT": i["L0_attn_in_proj_w"].T, "conv_blocks": blocks, "fc_wT": i["L0_attn_fc_w"].T,
        "cproj_w": i["L0_attn_cproj_w"], "out_wT": i["L0_attn_out_w"].T,
        "ln_g": col("L0_attn_ln_g"), "ln_b": col("L0_attn_ln_b"), "cproj_b": col("L0_attn_cproj_b"),
        "conv_b": col("L0_attn_conv_b"), "fc_b": col("L0_attn_fc_b"),
        **{n + "T": i["L0_ffn_" + n].T for n in ("wf", "wi", "wc", "wo", "uf", "ui", "uc", "uo")},
        **{n: col("L0_ffn_" + n) for n in ("bf", "bi", "bc", "bo", "in_c")},
        "wqT": np.asarray(i["L1_attn_w_qkv"])[:, 0:D].T, "w_qkv": i["L1_attn_w_qkv"], "w_out1": i["L1_attn_w_out"],
        "head_dirs": dirs, "head_scales": np.asarray(i["L1_attn_head_scales"]).reshape(HEADS, 1), "masks": masks,
        "w_r": i["L1_ffn_Wr"], "b_r": i["L1_ffn_br"], "w_up": w_up, "b_up": b_up, "w_down": w_down,
        "b_down": i["L1_ffn_b_down"],
        "trials": np.tile(units[:, None] * np.arange(1, 4, dtype=np.int32), (P, 1, 1)),
        "units": np.tile(units.astype(np.float32), (P, 1)), "same_expert": same.astype(np.float32),
        "before": before.astype(np.float32), "iota": np.tile(np.arange(P, dtype=np.float32), (P, 1)),
        "p_col": np.arange(P, dtype=np.float32)[:, None],
        "tile_no": np.tile((TT * np.arange(SEQ)[None, :] + np.arange(TT)[:, None]).astype(np.float32), (P, 1, 1)),
        "L0_cT": i["L0_c"].T, "L0_wmod": i["L0_wmod"], "L1_cT": i["L1_c"].T, "L1_wmod": i["L1_wmod"],
    }
    return {n: c(np.asarray(v)) for n, v in a.items()}


def kernel(**inputs):
    import concourse.bacc as bacc
    from concourse.bass_utils import run_bass_kernel_spmd

    arrays = _layout(inputs)
    nc = bacc.Bacc("TRN2", target_bir_lowering=False, num_devices=1)
    t = {n: nc.dram_tensor("in_" + n, a.shape, mybir.dt.from_np(a.dtype), kind="ExternalInput").ap()
         for n, a in arrays.items()}
    out = nc.dram_tensor("out", (NB, T, D), F32, kind="ExternalOutput").ap()
    program(nc, t, out)
    r = run_bass_kernel_spmd(nc, [{"in_" + n: a for n, a in arrays.items()}], core_ids=[0])
    return r.results[0]["out"]
```
